# Optimizing a Trainium2 kernel written in Bass

```python
import numpy as np
import jax
import jax.numpy as jnp

def _softmax(x, axis=-1):
    return jax.nn.softmax(x, axis=axis)

def _gelu(x):
    return jax.nn.gelu(x, approximate=True)

def _silu(x):
    return jax.nn.silu(x)

def _sigmoid(x):
    return jax.nn.sigmoid(x)

def _layernorm(x, axis=-1, eps=1e-05):
    m = jnp.mean(x, axis=axis, keepdims=True)
    v = jnp.var(x, axis=axis, keepdims=True)
    return (x - m) / jnp.sqrt(v + eps)

def _scatter_add(tgt, idx, src, axis=0):
    return tgt.at[idx].add(src)

def _segment_sum(src, seg, n):
    return jax.ops.segment_sum(src, seg, n)
kernel_name = 'mk_lm_tower_d2_tok_ids1024_r4_20c446'

def setup_inputs(seed: int=0):
    np.random.seed(seed)
    _w = jnp.asarray

    def _rec_inputs():
        import jax
        import jax.numpy as jnp
        _rk = jax.random.key(seed)
        x = jax.random.randint(jax.random.fold_in(_rk, 1), (16, 128), 0, 12564, jnp.int32)
        return x
    x = _rec_inputs()

    def _L0_tok_setup():
        import jax, jax.numpy as jnp
        import numpy as np
        VOCAB = 50257
        HIDDEN = 256
        BATCH = 4
        SEQ = 1024
        key = jax.random.key(seed)
        k_idx, k_w = jax.random.split(key)
        idx = jax.random.randint(k_idx, (BATCH, SEQ), 0, VOCAB, dtype=jnp.int64 if jax.config.jax_enable_x64 else jnp.int32)
        weight = jax.random.normal(k_w, (VOCAB, HIDDEN), dtype=jnp.float32)
        return {'idx': idx, 'weight': weight}
    _L0_tok_all = _L0_tok_setup()
    _L0_tok_in = {k: v for k, v in _L0_tok_all.items() if k in ('weight',)}
    del _L0_tok_all

    def _L0_attn_setup():
        import jax, jax.numpy as jnp
        import numpy as np
        NUM_HEADS = 16
        LN_EPS = 1e-05
        FEAT_EPS = 0.0001
        key = jax.random.key(seed)
        ks = jax.random.split(key, 4)
        B, L, D = (2, 512, 256)
        scale = 0.02
        return {'x': jax.random.normal(ks[0], (B, L, D), dtype=jnp.float32), 'Wqkv': jax.random.normal(ks[1], (3 * D, D), dtype=jnp.float32) * scale, 'bqkv': jnp.zeros((3 * D,), dtype=jnp.float32), 'Wout': jax.random.normal(ks[2], (D, D), dtype=jnp.float32) * scale, 'bout': jnp.zeros((D,), dtype=jnp.float32), 'gamma': jnp.ones((D,), dtype=jnp.float32), 'beta': jnp.zeros((D,), dtype=jnp.float32)}
    _L0_attn_all = _L0_attn_setup()
    _L0_attn_in = {k: v for k, v in _L0_attn_all.items() if k in ('Wqkv', 'bqkv', 'Wout', 'bout', 'gamma', 'beta')}
    del _L0_attn_all

    def _L0_ffn_setup():
        import jax, jax.numpy as jnp
        import numpy as np
        B, S, K, N = (8, 2048, 256, 256)
        key = jax.random.key(seed)
        k1, k2, k3, k4 = jax.random.split(key, 4)
        x = jax.random.normal(k1, (B, S, K), dtype=jnp.float32)
        CB = jnp.clip(jnp.round(jax.random.normal(k2, (N, K), dtype=jnp.float32) * 42.0), -127.0, 127.0)
        SCB = jax.random.uniform(k3, (N,), dtype=jnp.float32, minval=0.5, maxval=2.0)
        bias = jax.random.normal(k4, (N,), dtype=jnp.float32) * 0.02
        return {'x': x, 'CB': CB, 'SCB': SCB, 'bias': bias}
    _L0_ffn_all = _L0_ffn_setup()
    _L0_ffn_in = {k: v for k, v in _L0_ffn_all.items() if k in ('CB', 'SCB', 'bias')}
    del _L0_ffn_all

    def _L1_attn_setup():
        import jax, jax.numpy as jnp
        import numpy as np
        B, N, D_MODEL, HEADS, DFF, M = (4, 1024, 256, 16, 1024, 64)
        DH = D_MODEL // HEADS
        EPS_K = 0.0001
        LN_EPS = 1e-05

        def softmax_kernel(x, proj, is_query):
            norm = x.shape[-1] ** (-0.25)
            ratio = proj.shape[0] ** (-0.5)
            xp = jnp.einsum('bhnd,md->bhnm', x * norm, proj)
            diag = jnp.sum(jnp.square(x), axis=-1, keepdims=True) * 0.5 * (norm * norm)
            if is_query:
                stab = jnp.max(xp, axis=-1, keepdims=True)
            else:
                stab = jnp.max(xp, axis=(-1, -2), keepdims=True)
            return ratio * (jnp.exp(xp - diag - stab) + EPS_K)

        def layer_norm(x, g, b):
            mu = jnp.mean(x, axis=-1, keepdims=True)
            var = jnp.mean(jnp.square(x - mu), axis=-1, keepdims=True)
            return (x - mu) * jax.lax.rsqrt(var + LN_EPS) * g + b
        key = jax.random.key(seed)
        ks = jax.random.split(key, 12)
        s = 0.02
        return {'video': jax.random.normal(ks[0], (B, N, D_MODEL), jnp.float32), 'Wq': jax.random.normal(ks[1], (D_MODEL, D_MODEL), jnp.float32) * s, 'bq': jnp.zeros((D_MODEL,), jnp.float32), 'Wk': jax.random.normal(ks[2], (D_MODEL, D_MODEL), jnp.float32) * s, 'bk': jnp.zeros((D_MODEL,), jnp.float32), 'Wv': jax.random.normal(ks[3], (D_MODEL, D_MODEL), jnp.float32) * s, 'bv': jnp.zeros((D_MODEL,), jnp.float32), 'Wo': jax.random.normal(ks[4], (D_MODEL, D_MODEL), jnp.float32) * s, 'bo': jnp.zeros((D_MODEL,), jnp.float32), 'proj': jax.random.normal(ks[5], (M, DH), jnp.float32), 'W1': jax.random.normal(ks[6], (DFF, D_MODEL), jnp.float32) * s, 'b1': jnp.zeros((DFF,), jnp.float32), 'W2': jax.random.normal(ks[7], (D_MODEL, DFF), jnp.float32) * s, 'b2': jnp.zeros((D_MODEL,), jnp.float32), 'g2': jnp.ones((D_MODEL,), jnp.float32), 'be2': jnp.zeros((D_MODEL,), jnp.float32), 'g3': jnp.ones((D_MODEL,), jnp.float32), 'be3': jnp.zeros((D_MODEL,), jnp.float32)}
    _L1_attn_all = _L1_attn_setup()
    _L1_attn_in = {k: v for k, v in _L1_attn_all.items() if k in ('Wq', 'bq', 'Wk', 'bk', 'Wv', 'bv', 'Wo', 'bo', 'proj', 'W1', 'b1', 'W2', 'b2', 'g2', 'be2', 'g3', 'be3')}
    del _L1_attn_all

    def _L1_ffn_setup():
        import jax, jax.numpy as jnp
        import numpy as np
        S, B, D, FF, E = (256, 2, 256, 512, 8)
        key = jax.random.key(seed)
        ks = jax.random.split(key, 8)
        s = 0.02
        return {'hidden_states': jax.random.normal(ks[0], (S, B, D), dtype=jnp.float32), 'router_w': jax.random.normal(ks[1], (E, D), dtype=jnp.float32) * s, 'expert_gate': jax.random.normal(ks[2], (E, D, FF), dtype=jnp.float32) * s, 'expert_up': jax.random.normal(ks[3], (E, D, FF), dtype=jnp.float32) * s, 'expert_down': jax.random.normal(ks[4], (E, FF, D), dtype=jnp.float32) * s, 'shared_gate': jax.random.normal(ks[5], (D, FF), dtype=jnp.float32) * s, 'shared_up': jax.random.normal(ks[6], (D, FF), dtype=jnp.float32) * s, 'shared_down': jax.random.normal(ks[7], (FF, D), dtype=jnp.float32) * s}
    _L1_ffn_all = _L1_ffn_setup()
    _L1_ffn_in = {k: v for k, v in _L1_ffn_all.items() if k in ('router_w', 'expert_gate', 'expert_up', 'expert_down', 'shared_gate', 'shared_up', 'shared_down')}
    del _L1_ffn_all
    return {'x': x, 'L0_tok_weight': _L0_tok_in['weight'], 'L0_attn_Wqkv': _L0_attn_in['Wqkv'], 'L0_attn_bqkv': _L0_attn_in['bqkv'], 'L0_attn_Wout': _L0_attn_in['Wout'], 'L0_attn_bout': _L0_attn_in['bout'], 'L0_attn_gamma': _L0_attn_in['gamma'], 'L0_attn_beta': _L0_attn_in['beta'], 'L0_ffn_CB': _L0_ffn_in['CB'], 'L0_ffn_SCB': _L0_ffn_in['SCB'], 'L0_ffn_bias': _L0_ffn_in['bias'], 'L1_attn_Wq': _L1_attn_in['Wq'], 'L1_attn_bq': _L1_attn_in['bq'], 'L1_attn_Wk': _L1_attn_in['Wk'], 'L1_attn_bk': _L1_attn_in['bk'], 'L1_attn_Wv': _L1_attn_in['Wv'], 'L1_attn_bv': _L1_attn_in['bv'], 'L1_attn_Wo': _L1_attn_in['Wo'], 'L1_attn_bo': _L1_attn_in['bo'], 'L1_attn_proj': _L1_attn_in['proj'], 'L1_attn_W1': _L1_attn_in['W1'], 'L1_attn_b1': _L1_attn_in['b1'], 'L1_attn_W2': _L1_attn_in['W2'], 'L1_attn_b2': _L1_attn_in['b2'], 'L1_attn_g2': _L1_attn_in['g2'], 'L1_attn_be2': _L1_attn_in['be2'], 'L1_attn_g3': _L1_attn_in['g3'], 'L1_attn_be3': _L1_attn_in['be3'], 'L1_ffn_router_w': _L1_ffn_in['router_w'], 'L1_ffn_expert_gate': _L1_ffn_in['expert_gate'], 'L1_ffn_expert_up': _L1_ffn_in['expert_up'], 'L1_ffn_expert_down': _L1_ffn_in['expert_down'], 'L1_ffn_shared_gate': _L1_ffn_in['shared_gate'], 'L1_ffn_shared_up': _L1_ffn_in['shared_up'], 'L1_ffn_shared_down': _L1_ffn_in['shared_down']}

def reference(x, L0_tok_weight, L0_attn_Wqkv, L0_attn_bqkv, L0_attn_Wout, L0_attn_bout, L0_attn_gamma, L0_attn_beta, L0_ffn_CB, L0_ffn_SCB, L0_ffn_bias, L1_attn_Wq, L1_attn_bq, L1_attn_Wk, L1_attn_bk, L1_attn_Wv, L1_attn_bv, L1_attn_Wo, L1_attn_bo, L1_attn_proj, L1_attn_W1, L1_attn_b1, L1_attn_W2, L1_attn_b2, L1_attn_g2, L1_attn_be2, L1_attn_g3, L1_attn_be3, L1_ffn_router_w, L1_ffn_expert_gate, L1_ffn_expert_up, L1_ffn_expert_down, L1_ffn_shared_gate, L1_ffn_shared_up, L1_ffn_shared_down):
    import jax
    import jax.numpy as jnp

    def _L0_tok_ref(idx, weight):
        import jax, jax.numpy as jnp
        import numpy as np
        VOCAB = 50257
        HIDDEN = 256
        BATCH = 4
        SEQ = 1024
        return jnp.take(weight, idx, axis=0)

    def _L0_attn_ref(x, Wqkv, bqkv, Wout, bout, gamma, beta):
        import jax, jax.numpy as jnp
        import numpy as np
        NUM_HEADS = 16
        LN_EPS = 1e-05
        FEAT_EPS = 0.0001
        B, L, D = x.shape
        H = NUM_HEADS
        E = D // H
        qkv = x @ Wqkv.T + bqkv
        q, k, v = jnp.split(qkv, 3, axis=-1)
        q = q.reshape(B, L, H, E)
        k = k.reshape(B, L, H, E)
        v = v.reshape(B, L, H, E)
        q = (jax.nn.elu(q) + 1.0 + FEAT_EPS) / jnp.sqrt(jnp.asarray(E, q.dtype))
        k = jax.nn.elu(k) + 1.0 + FEAT_EPS
        kv = jnp.einsum('blhe,blhf->blhef', k, v)
        kv_cumsum = jnp.cumsum(kv, axis=1)
        k_cumsum = jnp.cumsum(k, axis=1)
        num = jnp.einsum('blhe,blhef->blhf', q, kv_cumsum)
        den = jnp.einsum('blhe,blhe->blh', q, k_cumsum)[..., None] + FEAT_EPS
        out = (num / den).reshape(B, L, D)
        out = out @ Wout.T + bout
        mu = jnp.mean(out, axis=-1, keepdims=True)
        var = jnp.var(out, axis=-1, keepdims=True)
        return (out - mu) / jnp.sqrt(var + LN_EPS) * gamma + beta

    def _L0_ffn_ref(x, CB, SCB, bias):
        import jax, jax.numpy as jnp
        import numpy as np
        B, S, K, N = (8, 2048, 256, 256)
        out = jnp.einsum('bsk,nk->bsn', x, CB)
        out = out * (SCB * (1.0 / 127.0)) + bias
        return out

    def _L1_attn_ref(video, Wq, bq, Wk, bk, Wv, bv, Wo, bo, proj, W1, b1, W2, b2, g2, be2, g3, be3):
        import jax, jax.numpy as jnp
        import numpy as np
        B, N, D_MODEL, HEADS, DFF, M = (4, 1024, 256, 16, 1024, 64)
        DH = D_MODEL // HEADS
        EPS_K = 0.0001
        LN_EPS = 1e-05

        def softmax_kernel(x, proj, is_query):
            norm = x.shape[-1] ** (-0.25)
            ratio = proj.shape[0] ** (-0.5)
            xp = jnp.einsum('bhnd,md->bhnm', x * norm, proj)
            diag = jnp.sum(jnp.square(x), axis=-1, keepdims=True) * 0.5 * (norm * norm)
            if is_query:
                stab = jnp.max(xp, axis=-1, keepdims=True)
            else:
                stab = jnp.max(xp, axis=(-1, -2), keepdims=True)
            return ratio * (jnp.exp(xp - diag - stab) + EPS_K)

        def layer_norm(x, g, b):
            mu = jnp.mean(x, axis=-1, keepdims=True)
            var = jnp.mean(jnp.square(x - mu), axis=-1, keepdims=True)
            return (x - mu) * jax.lax.rsqrt(var + LN_EPS) * g + b
        b, n, d = video.shape
        split = lambda t: t.reshape(b, n, HEADS, DH).transpose(0, 2, 1, 3)
        q = split(video @ Wq.T + bq)
        k = split(video @ Wk.T + bk)
        v = split(video @ Wv.T + bv)
        qp = softmax_kernel(q, proj, is_query=True)
        kp = softmax_kernel(k, proj, is_query=False)
        k_sum = jnp.sum(kp, axis=2)
        denom = jnp.einsum('bhnm,bhm->bhn', qp, k_sum)
        ctx = jnp.einsum('bhnm,bhnd->bhmd', kp, v)
        out = jnp.einsum('bhnm,bhmd->bhnd', qp, ctx) / denom[..., None]
        attn = out.transpose(0, 2, 1, 3).reshape(b, n, d) @ Wo.T + bo
        x = layer_norm(video + attn, g2, be2)
        ff = jax.nn.relu(x @ W1.T + b1) @ W2.T + b2
        return layer_norm(x + ff, g3, be3)

    def _L1_ffn_ref(hidden_states, router_w, expert_gate, expert_up, expert_down, shared_gate, shared_up, shared_down):
        import jax, jax.numpy as jnp
        import numpy as np
        S, B, D, FF, E = (256, 2, 256, 512, 8)
        seq, bs, d = hidden_states.shape
        n_experts = expert_gate.shape[0]
        x = hidden_states.reshape(-1, d)
        logits = jnp.einsum('td,ed->te', x, router_w)
        top_logit = jnp.max(logits, axis=-1)
        top_idx = jnp.argmax(logits, axis=-1)
        score = jax.nn.sigmoid(top_logit)
        onehot = jax.nn.one_hot(top_idx, n_experts, dtype=x.dtype)
        xs = x * score[:, None]
        g = jnp.einsum('td,edf->etf', xs, expert_gate)
        u = jnp.einsum('td,edf->etf', xs, expert_up)
        h = jax.nn.silu(g) * u
        eo = jnp.einsum('etf,efd->etd', h, expert_down)
        moe_out = jnp.einsum('te,etd->td', onehot, eo)
        sh = jax.nn.silu(x @ shared_gate) * (x @ shared_up) @ shared_down
        return (moe_out + sh).reshape(seq, bs, d)
    h = _L0_tok_ref(x, L0_tok_weight)
    h = h + _L0_attn_ref(_layernorm(h, axis=-1), L0_attn_Wqkv, L0_attn_bqkv, L0_attn_Wout, L0_attn_bout, L0_attn_gamma, L0_attn_beta)
    h = h + _L0_ffn_ref(_layernorm(h, axis=-1), L0_ffn_CB, L0_ffn_SCB, L0_ffn_bias)
    h = h + _L1_attn_ref(_layernorm(h, axis=-1), L1_attn_Wq, L1_attn_bq, L1_attn_Wk, L1_attn_bk, L1_attn_Wv, L1_attn_bv, L1_attn_Wo, L1_attn_bo, L1_attn_proj, L1_attn_W1, L1_attn_b1, L1_attn_W2, L1_attn_b2, L1_attn_g2, L1_attn_be2, L1_attn_g3, L1_attn_be3)
    h = h + _L1_ffn_ref(_layernorm(h, axis=-1), L1_ffn_router_w, L1_ffn_expert_gate, L1_ffn_expert_up, L1_ffn_expert_down, L1_ffn_shared_gate, L1_ffn_shared_up, L1_ffn_shared_down)
    return h

_drawn_inputs = setup_inputs


def setup_inputs(seed=0):
    import zlib

    import numpy as np

    out = dict(_drawn_inputs(seed))
    spreads = {'L0_attn_bqkv': (0.0, 0.1),
     'L0_attn_bout': (0.0, 0.1),
     'L0_attn_gamma': (1.0, 0.2),
     'L0_attn_beta': (0.0, 0.1),
     'L1_attn_bq': (0.0, 2.0),
     'L1_attn_bk': (0.0, 2.0),
     'L1_attn_bv': (0.0, 0.8),
     'L1_attn_bo': (0.0, 0.654),
     'L1_attn_b1': (0.0, 0.8),
     'L1_attn_b2': (0.0, 0.679),
     'L1_attn_g2': (1.0, 0.6),
     'L1_attn_be2': (0.0, 0.677),
     'L1_attn_g3': (1.0, 0.561),
     'L1_attn_be3': (0.0, 0.699)}
    factors = {'L0_ffn_bias': 8.0,
     'L1_attn_Wq': 64.0,
     'L1_attn_Wk': 64.0,
     'L1_attn_Wv': 7.023,
     'L1_attn_Wo': 6.362,
     'L1_attn_proj': 64.0,
     'L1_attn_W1': 3.872,
     'L1_attn_W2': 3.055,
     'L1_ffn_router_w': 8.0,
     'L1_ffn_expert_gate': 8.0,
     'L1_ffn_expert_up': 8.0,
     'L1_ffn_expert_down': 8.0,
     'L1_ffn_shared_gate': 8.0,
     'L1_ffn_shared_up': 8.0,
     'L1_ffn_shared_down': 8.0}
    for name, (base, spread) in spreads.items():
        noise = np.random.default_rng([zlib.crc32(name.encode()), seed]).standard_normal(out[name].shape)
        drawn = base * np.exp(spread * noise) if base else spread * noise
        out[name] = jnp.asarray(drawn.astype(out[name].dtype))
    for name, factor in factors.items():
        out[name] = (out[name] * factor).astype(out[name].dtype)
    return out
```

```python
from contextlib import ExitStack

import concourse.bass as bass
from concourse import mybir

ALU = mybir.AluOpType
ACT = mybir.ActivationFunctionType
AX = mybir.AxisListType
F32 = mybir.dt.float32
U32 = mybir.dt.uint32
MAX = bass.bass_isa.ReduceOp.max

P = 128
MOE_SLOTS = 2
PIECES = 3
LN, TR = 7, 7
A, B, C = range(PIECES)
GATHERED_ALONE = 3
LINKS = [15, 10, 11]
LN_EPS = 1e-5
FEAT_EPS = 1e-4
EPS_K = 1e-4

ROWS = ["v0_bias", "out0_bias", "gamma0", "beta0", "ffn0_scb", "ffn0_bias",
        "v1_bias", "out1_bias", "g2", "be2", "b2", "g3", "be3"]


def bass_lm_tower(nc, idx, table, w_qk0, w_v0, w_out0, cb, w_qk1, w_v1, w_out1, proj, w_ff1, w_ff2,
                  w_router, w_shared_gate, w_shared_up, w_shared_down, w_experts, rows, cols, ident, causal,
                  head_sum, before, out):
    D = table.shape[1]
    T = idx.shape[1]
    KD = D // P
    HEADS, DH = 16, D // 16
    PAIRS = HEADS // 2
    M = proj.shape[1]
    FF1 = w_ff1.shape[2]
    KF = FF1 // P
    F = w_shared_gate.shape[2]
    KE = F // P
    E = w_router.shape[2]
    V1 = DH + 1
    EXPERT = w_experts.shape[2]
    SORTED_TILES = T + E
    GATE, UP, DOWN = 0, KD * F, 2 * KD * F
    RESIDENT = 3
    with ExitStack() as ctx:
        def sb(name, shape, dt=F32):
            return ctx.enter_context(nc.sbuf_tensor(name, shape, dt))

        def sem(name):
            return ctx.enter_context(nc.semaphore(name))

        we = sb("we", [P, E * EXPERT])
        H = sb("H", [P, T, D])
        Y = sb("Y", [P, T, D])
        logits = sb("logits", [P, T, E])
        idx_sb = sb("idx_sb", [P, T], U32)
        id_sb = sb("id_sb", [P, P])
        before_sb = sb("before_sb", [P, P])
        ones_sb = sb("ones_sb", [P, P])
        pow_half = sb("pow_half", [P, 1])
        ln_eps = sb("ln_eps", [P, 1])
        cols_sb = sb("cols_sb", [P, cols.shape[1]])
        spare = [RESIDENT * EXPERT, E * EXPERT]

        def overlaid(k, n):
            at = spare[0]
            spare[0] += k * n
            assert spare[0] <= spare[1]
            return we[:, at:at + k * n].rearrange("p (k n) -> p k n", k=k)

        ff1_sb, ff2_sb = overlaid(KD, FF1), overlaid(KF, D)
        qk0_sb, qk1_sb = overlaid(KD, 2 * D), overlaid(KD, 2 * D)
        sg_sb, su_sb = overlaid(KD, F), overlaid(KD, F)
        sd_sb = overlaid(KE, D)
        v0_sb, v1w_sb, out0_sb, out1_sb, cb_sb = (overlaid(KD, D) for _ in range(5))
        router_sb = sb("router_sb", [P, KD, E])
        proj_sb = sb("proj_sb", [P, 8 * M])
        rows_sb = overlaid(len(ROWS), D)
        causal_sb = sb("causal_sb", [P, P])
        hsum_sb = sb("hsum_sb", [P, 8])
        row = {n: rows_sb[:, i, :] for i, n in enumerate(ROWS)}
        qk0_bias, qk1_bias, b1_col, parity = (cols_sb[:, 0:4], cols_sb[:, 4:8], cols_sb[:, 8:8 + KF],
                                              cols_sb[:, 8 + KF:10 + KF])
        yA, tmpA, preA = sb("yA", [P, D]), sb("tmpA", [P, D]), sb("preA", [P, D])
        yTA = sb("yTA", [P, KD, P])
        qkA = sb("qkA", [P, 4, P])
        xA = sb("xA", [P, 4, P])
        qz = sb("qz", [P, KD, 2, P])
        voA = sb("voA", [P, HEADS, V1])
        S_sb = sb("S_sb", [P, 4, 4, P])
        yB, tmpB, preB = sb("yB", [P, D]), sb("tmpB", [P, D]), sb("preB", [P, D])
        yTB = sb("yTB", [P, KD, P])
        qkB = sb("qkB", [P, 4, P])
        sqB = sb("sqB", [P, 4, P])
        voB = sb("voB", [P, HEADS, V1])
        kf = sb("kf", [P, HEADS, M])
        qf = sb("qf", [P, HEADS, M])
        qfT = sb("qfT", [P, PAIRS, P])
        ctxbd = sb("ctxbd", [P, PAIRS, 2 * V1])
        x1, yC, tmpC, preC = sb("x1", [P, D]), sb("yC", [P, D]), sb("tmpC", [P, D]), sb("preC", [P, D])
        yTC = sb("yTC", [P, KD, P])
        ffT = sb("ffT", [P, KF, P])
        gC = sb("gC", [P, F])
        tC = sb("tC", [P, F])
        hT = sb("hT", [P, KE, P])
        stats = sb("stats", [P, 7, 6])
        mv = sb("mv", [P, 7, 2])
        rstd = sb("rstd", [P, 7, 2])
        denA = sb("denA", [P, 2, HEADS])
        denB = sb("denB", [P, 2, HEADS])
        diag = sb("diag", [P, 2, HEADS])
        kmax = sb("kmax", [P, 3, HEADS])
        qmax = sb("qmax", [P, 2, HEADS])
        top = sb("top", [P, 4])
        psA = ctx.enter_context(nc.psum_tensor("psA", [P, 3, 512], F32))
        psB = ctx.enter_context(nc.psum_tensor("psB", [P, 3, 512], F32))
        psC = ctx.enter_context(nc.psum_tensor("psC", [P, 2, 512], F32))
        rt = sb("rt", [P, 4 * E + SORTED_TILES + 8])
        flatS = S_sb[:].rearrange("p b a n -> p (b a n)")
        ra, rb, onehot, counts = (flatS[:, n * T * E:(n + 1) * T * E].rearrange("p (t e) -> p t e", t=T)
                                  for n in range(4))
        slot_u = sb("slot_u", [P, T], U32)
        tile_expert_t = sb("tile_expert", [P, SORTED_TILES], mybir.dt.int32)
        tile_expert = tile_expert_t[:]
        Yz = sb("Yz", [P, D])

        Y_zero = Yz[:].unsqueeze(1).broadcast_to([P, SORTED_TILES, D])
        xs_dram = nc.dram_tensor("xs_sorted", [SORTED_TILES * P, D], F32, kind="Internal").ap()
        ys_dram = nc.dram_tensor("ys_sorted", [SORTED_TILES * P, D], F32, kind="Internal").ap()

        names = """idx_loaded small_loaded vectors_loaded zero_ready consts_ready gathered_rest
        block0_loaded middle_loaded last_loaded proj_loaded proj_scaled
        experts_loaded late_loaded zeros_stored
        qk0_psum v0_psum xmin_ready exp_ready qk0_ready v0_ready scores_psum scores_masked heads0_psum
        out0_psum preA_ready hA_ready
        ffn0_psum preA2_ready qk1_psum v1_psum qk1_ready v1_ready square_ready diag_psum diag_read
        xk_psum xk_read kmax_ready kmax_all kexp_in kexp_out kfeat_ready xq_psum qexp_in qfeat_ready
        qT_psum qT_ready ctx_psum ctx_ready heads1_psum preB_ready out1_psum
        x1_ready preC_ready hC_ahead ff1_psum ff_ready ff2_psum
        logit_psum logit_read tanh_top gate_psum up_psum tanh_gate hT_ready down_psum tile_done
        onehot_ready count_psum slots_ready xs_scattered xT_psum xT_ready eg_psum eu_psum
        tanh_eg eh_ready ehT_psum ehT_ready ey_psum ey_ready ey_free eg_ready added out_stored
        pool_step routing_step unused unused2""".split()
        S = {n: sem(n) for n in names}
        var_ready = [sem(f"var{k}_ready") for k in range(LN)]
        rstd_ready = [sem(f"rstd{k}_ready") for k in range(LN)]
        src_ready = [sem(f"src{k}_ready") for k in range(TR)]
        srcT_psum = [sem(f"src{k}T_psum") for k in range(TR)]
        srcT_ready = [sem(f"src{k}T_ready") for k in range(TR)]
        dve_step = [sem(f"dve_step_{x}") for x in "ABC"]
        gathered = [sem(f"gathered{t}") for t in range(GATHERED_ALONE)]
        x_loaded = [sem(f"x_loaded{s}") for s in range(MOE_SLOTS)]
        ey_stored = [sem(f"ey_stored{s}") for s in range(MOE_SLOTS)]
        fetched = [sem(f"fetched{q}") for q in range(4)]

        xm = [yA[:], yB[:]]
        xT = [yTA[:], yTB[:]]
        eg1 = [kf[:].rearrange("p h m -> p (h m)")[:, 0:F], qf[:].rearrange("p h m -> p (h m)")[:, 0:F]]
        eg2 = [kf[:].rearrange("p h m -> p (h m)")[:, F:2 * F], qf[:].rearrange("p h m -> p (h m)")[:, F:2 * F]]
        eh = [xA[:], sqB[:]]
        ehT = [qkA[:], qkB[:]]
        ey = [tmpA[:], tmpB[:]]
        banks_of = [[psA[:, 0, :], psA[:, 1, :], psA[:, 2, :], psC[:, 0, :]],
                    [psB[:, 0, :], psB[:, 1, :], psB[:, 2, :], psC[:, 1, :]]]

        def flat(v):
            return v.rearrange("p a n -> p (a n)")

        def by4(v):
            return v.rearrange("p (a n) -> p a n", a=4)

        def heads(b):
            return b[:, 0:HEADS * V1].rearrange("p (h v) -> p h v", h=HEADS)

        def chunk_bias(col, n):
            return col.unsqueeze(2).broadcast_to([P, n, P])

        def by_head(v, n):
            return v.unsqueeze(2).broadcast_to([P, HEADS, n])

        def run_steps(engine, order):
            def step(u, active):
                for p, stage in order:
                    if p in active:
                        stage(u - p)

            for u in range(PIECES - 1):
                step(u, range(u + 1))
            with engine.Fori(PIECES - 1, T) as u:
                step(u, range(PIECES))
            for u in range(T, T + PIECES - 1):
                step(u, range(u - T + 1, PIECES))

        block = ctx.enter_context(nc.Block())

        @block.sync
        def _(sp):
            sp.dma_start(idx_sb[:], idx).then_inc(S["idx_loaded"], 16)
            for dst, src in ((id_sb[:], ident), (cols_sb[:], cols)):
                sp.dma_start(dst, src).then_inc(S["small_loaded"], 16)
            for dst, src in ((qk0_sb, w_qk0), (v0_sb, w_v0)):
                sp.dma_start(dst, src).then_inc(S["block0_loaded"], 16)
            sp.dma_start(rows_sb, rows.partition_broadcast(P)).then_inc(S["vectors_loaded"], 16)
            sp.dma_start(causal_sb[:], causal).then_inc(S["block0_loaded"], 16)
            sp.dma_start(out0_sb, w_out0).then_inc(S["block0_loaded"], 16)
            sp.wait_ge(S["zero_ready"], 4)
            for h in range(8):
                sp.dma_start(proj_sb[DH * h:DH * h + DH, M * h:M * h + M], proj).then_inc(S["proj_loaded"], 16)
            for dst, src in ((cb_sb, cb), (qk1_sb, w_qk1), (v1w_sb, w_v1), (hsum_sb[:], head_sum), (out1_sb, w_out1)):
                sp.dma_start(dst, src).then_inc(S["middle_loaded"], 16)
            for dst, src in ((ff1_sb, w_ff1), (ff2_sb, w_ff2), (router_sb[:], w_router), (sg_sb, w_shared_gate),
                             (su_sb, w_shared_up), (sd_sb, w_shared_down), (before_sb[:], before)):
                sp.dma_start(dst, src).then_inc(S["last_loaded"], 16)
            sp.dma_start(xs_dram.rearrange("(j p) d -> p j d", p=P), Y_zero).then_inc(S["zeros_stored"], 16)
            for e in range(RESIDENT):
                sp.dma_start(we[:, e * EXPERT:(e + 1) * EXPERT], w_experts[e]).then_inc(S["experts_loaded"], 16)
            sp.wait_ge(S["tile_done"], T)
            for e in range(RESIDENT, E):
                sp.dma_start(we[:, e * EXPERT:(e + 1) * EXPERT], w_experts[e]).then_inc(S["late_loaded"], 16)
            sp.wait_ge(S["xs_scattered"], 16 * T)
            for s in range(MOE_SLOTS):
                sp.dma_start(xm[s], xs_dram[s * P:(s + 1) * P, :]).then_inc(x_loaded[s], 16)
            with sp.Fori(0, SORTED_TILES // MOE_SLOTS - 1) as i:
                for s in range(MOE_SLOTS):
                    j = i * MOE_SLOTS + s
                    sp.wait_ge(S["xT_psum"], j + 1)
                    sp.dma_start(xm[s], xs_dram[bass.ts(j + MOE_SLOTS, P), :]).then_inc(x_loaded[s], 16)
            for q in range(4):
                n = T // 4
                sp.wait_ge(S["added"], q + 1)
                sp.dma_start(out[q * n:(q + 1) * n].rearrange("t p d -> p t d"),
                             H[:, q * n:(q + 1) * n, :]).then_inc(S["out_stored"], 16)
            sp.wait_ge(S["out_stored"], 16 * 4)

        @block.gpsimd
        def _(pool):
            pool.wait_ge(S["idx_loaded"], 16)
            for t in range(T):
                pool.indirect_dma_start(out=H[:, t, :], out_offset=None, in_=table,
                                        in_offset=bass.IndirectOffsetOnAxis(ap=idx_sb[:, t:t + 1], axis=0)
                                        ).then_inc(gathered[t] if t < GATHERED_ALONE else S["gathered_rest"], 16)
                if t == 1:
                    pool.memset(pow_half[:], -0.5).then_inc(S["zero_ready"], 1)
                    pool.memset(ln_eps[:], LN_EPS).then_inc(S["zero_ready"], 1)
                    pool.memset(proj_sb[:], 0.0).then_inc(S["zero_ready"], 1)
                    pool.memset(Yz[:], 0.0).then_inc(S["zero_ready"], 1)
                    pool.memset(ones_sb[:], 1.0).then_inc(S["consts_ready"], 1)
                    pool.memset(ctxbd[:], 0.0).then_inc(S["consts_ready"], 1)
                    pool.memset(voA[:], 1.0).then_inc(S["consts_ready"], 1)
                    pool.memset(voB[:], 1.0).then_inc(S["consts_ready"], 1)
            pool.wait_ge(S["zero_ready"], 4)

            def inverse_deviation(k):
                def stage(t):
                    pool.wait_ge(var_ready[k], t + 1)
                    pool.tensor_tensor(rstd[:, k, 0:1], mv[:, k, 1:2], ln_eps[:], ALU.add).then_inc(pool_ln[k], 1)
                    pool.wait_ge(pool_ln[k], t + 1)
                    pool.tensor_tensor(rstd[:, k, 1:2], rstd[:, k, 0:1], pow_half[:],
                                       ALU.pow).then_inc(rstd_ready[k], 1)
                return stage

            def ahead_A(t):
                if isinstance(t, int):
                    pool.wait_ge(S["vectors_loaded"], 16)
                    pool.wait_ge(gathered[t] if t < GATHERED_ALONE else S["gathered_rest"],
                                 16 if t < GATHERED_ALONE else 16 * (T - GATHERED_ALONE))
                else:
                    pool.wait_ge(S["gathered_rest"], 16 * (T - GATHERED_ALONE))
                pool.tensor_tensor(preA[:], H[:, t, :], row["beta0"], ALU.add).then_inc(S["preA_ready"], 1)

            def ahead_A2(t):
                pool.tensor_tensor(preA[:], H[:, t, :], row["ffn0_bias"], ALU.add).then_inc(S["preA2_ready"], 1)

            def ahead_B(t):
                pool.wait_ge(src_ready[3], t + 1)
                pool.tensor_tensor(preB[:], yB[:], row["out1_bias"], ALU.add).then_inc(S["preB_ready"], 1)

            def reduce_kmax(t):
                pool.wait_ge(S["kmax_ready"], t + 1)
                pool.sem_inc(S["unused"], 1)
                pool.partition_all_reduce(kmax[:, 1, :], kmax[:, 0, :], P, MAX).then_inc(S["kmax_all"], 1)

            def ahead_C(t):
                pool.wait_ge(S["x1_ready"], t + 1)
                pool.tensor_tensor(preC[:], x1[:], row["b2"], ALU.add).then_inc(S["preC_ready"], 1)
                pool.tensor_tensor(H[:, t, :], H[:, t, :], row["be3"], ALU.add).then_inc(S["hC_ahead"], 1)

            pool_ln = [sem(f"pool_ln{k}") for k in range(LN)]
            run_steps(pool, [
                (B, inverse_deviation(3)), (A, inverse_deviation(0)), (A, ahead_A), (C, ahead_C), (B, ahead_B),
                (B, reduce_kmax), (C, inverse_deviation(5)), (C, inverse_deviation(6)), (A, inverse_deviation(1)),
                (A, inverse_deviation(2)), (B, inverse_deviation(4)), (A, ahead_A2),
            ])

            pool.wait_ge(S["zeros_stored"], 16)
            pool.wait_ge(S["slots_ready"], 1)
            for t in range(T):
                pool.indirect_dma_start(out=xs_dram, out_offset=bass.IndirectOffsetOnAxis(ap=slot_u[:, t:t + 1], axis=0),
                                        in_=Y[:, t, :], in_offset=None).then_inc(S["xs_scattered"], 16)
            pool.sem_inc(S["ey_free"], MOE_SLOTS)
            with pool.Fori(0, SORTED_TILES // MOE_SLOTS) as i:
                for s in range(MOE_SLOTS):
                    j = i * MOE_SLOTS + s
                    pool.wait_ge(S["ey_ready"], j + 1)
                    pool.dma_start(ys_dram[bass.ts(j, P), :], ey[s]).then_inc(ey_stored[s], 16)
                for s in range(MOE_SLOTS):
                    pool.wait_ge(ey_stored[s], i * 16 + 16)
                    pool.sem_inc(S["ey_free"], 1)
            for t in range(T):
                q = t // (T // 4)
                pool.indirect_dma_start(out=Y[:, t, :], out_offset=None, in_=ys_dram,
                                        in_offset=bass.IndirectOffsetOnAxis(ap=slot_u[:, t:t + 1], axis=0)
                                        ).then_inc(fetched[q], 16)

        @block.scalar
        def _(act):
            def operand(k, dst, src):
                def stage(t):
                    act.wait_ge(srcT_psum[k], t + 1)
                    act.activation(flat(dst[:]), src[:, 0:D], ACT.Copy).then_inc(srcT_ready[k], 1)
                return stage

            def exp_min(t):
                act.wait_ge(S["xmin_ready"], t + 1)
                act.activation(qz[:].rearrange("p a b n -> p (a b n)"), qz[:].rearrange("p a b n -> p (a b n)"),
                               ACT.Exp).then_inc(S["exp_ready"], 1)

            def square(t):
                act.wait_ge(S["qk1_ready"], t + 1)
                act.activation(flat(sqB[:]), flat(qkB[:]), ACT.Square).then_inc(S["square_ready"], 1)

            def read_xk(t):
                act.wait_ge(S["xk_psum"], t + 1)
                act.activation(flat(kf[:]), psB[:, 1:3, :].rearrange("p b n -> p (b n)"), ACT.Copy
                               ).then_inc(S["xk_read"], 1)

            def exp_q(t):
                act.wait_ge(S["qexp_in"], t + 1)
                act.activation(flat(qf[:]), flat(qf[:]), ACT.Exp).then_inc(S["qfeat_ready"], 1)

            def exp_k(t):
                act.wait_ge(S["kexp_in"], t + 1)
                act.activation(flat(kf[:]), flat(kf[:]), ACT.Exp).then_inc(S["kexp_out"], 1)

            def read_qT(t):
                act.wait_ge(S["qT_psum"], t + 1)
                act.activation(flat(qfT[:]), psB[:, 0:2, :].rearrange("p b n -> p (b n)"),
                               ACT.Copy, bias=EPS_K).then_inc(S["qT_ready"], 1)

            def relu(half):
                def stage(t):
                    act.wait_ge(S["ff1_psum"], t * 2 + (half + 1))
                    for f in range(4 * half, 4 * half + 4):
                        act.activation(ffT[:, f, :], psC[:, 1 - half, f % 4 * P:f % 4 * P + P], ACT.Relu,
                                       bias=b1_col[:, f:f + 1]).then_inc(S["ff_ready"], 1)
                return stage

            def tanh_top(t):
                act.wait_ge(S["logit_read"], t + 1)
                act.activation(top[:, 1:2], top[:, 0:1], ACT.Tanh, scale=0.5).then_inc(S["tanh_top"], 1)

            def tanh_gate(t):
                act.wait_ge(S["gate_psum"], t + 1)
                act.activation(tC[:], psC[:, 0, :], ACT.Tanh, scale=0.5).then_inc(S["tanh_gate"], 1)

            act.wait_ge(S["small_loaded"], 16 * 2)
            run_steps(act, [
                (C, operand(5, yTC, psC[:, 0, :])), (B, operand(3, yTB, psB[:, 0, :])),
                (A, operand(0, yTA, psA[:, 0, :])), (B, square), (A, exp_min), (B, read_xk), (C, relu(0)),
                (C, relu(1)), (B, exp_q), (B, exp_k), (A, operand(1, yTA, psA[:, 2, :])), (B, read_qT),
                (C, operand(6, yTC, psC[:, 0, :])), (C, tanh_top), (B, operand(4, yTB, psB[:, 0, :])), (C, tanh_gate),
                (A, operand(2, yTA, psA[:, 0, :])),
            ])

            with act.Fori(0, SORTED_TILES // MOE_SLOTS) as i:
                for s in range(MOE_SLOTS):
                    act.wait_ge(S["xT_psum"], i * MOE_SLOTS + s + 1)
                    act.activation(flat(xT[s]), banks_of[s][0][:, 0:D], ACT.Copy).then_inc(S["xT_ready"], 1)
                for s in range(MOE_SLOTS):
                    act.wait_ge(S["eg_psum"], i * MOE_SLOTS + s + 1)
                    act.activation(eg1[s], banks_of[s][1], ACT.Tanh, scale=0.5).then_inc(S["tanh_eg"], 1)
                for s in range(MOE_SLOTS):
                    act.wait_ge(S["ehT_psum"], i * MOE_SLOTS + s + 1)
                    act.activation(flat(ehT[s]), banks_of[s][3], ACT.Copy).then_inc(S["ehT_ready"], 1)

        @block.vector
        def _(dve):
            links = [0, 0, 0]

            def link(p, t, ins):
                links[p] += 1
                ins.then_inc(dve_step[p], 1)
                dve.wait_ge(dve_step[p], t * LINKS[p] + links[p])

            def begins(p):
                assert links[p] in (0, LINKS[p]), (p, links)
                links[p] = 0

            def norm_stats(k, p, src, t):
                dve.sem_inc(S["unused"], 1)
                link(p, t, dve.bn_stats(stats[:, k], src))
                dve.sem_inc(S["unused"], 1)
                dve.bn_aggr(mv[:, k], stats[:, k]).then_inc(var_ready[k], 1)

            def normalise(dst, src, k, t):
                dve.wait_ge(rstd_ready[k], t + 1)
                return dve.tensor_scalar(dst, src, mv[:, k, 0:1], rstd[:, k, 1:2], ALU.subtract, ALU.mult)

            def weighted_mean(p, t, bank, den, eps, dst, k):
                h = heads(bank)
                link(p, t, dve.tensor_scalar(den[:, 0, :], h[:, :, DH], eps, None, ALU.add))
                link(p, t, dve.reciprocal(den[:, 1, :], den[:, 0, :]))
                dve.tensor_tensor(dst[:].rearrange("p (h c) -> p h c", h=HEADS), h[:, :, 0:DH],
                                  by_head(den[:, 1, :], DH), ALU.mult).then_inc(src_ready[k], 1)

            def values(dst, bank, bias, done):
                dve.tensor_tensor(dst[:, :, 0:DH], bank[:, 0:D].rearrange("p (h c) -> p h c", h=HEADS),
                                  bias.rearrange("p (h c) -> p h c", h=HEADS), ALU.add).then_inc(S[done], 1)

            def a_stats(t):
                begins(0)
                if isinstance(t, int) and t < GATHERED_ALONE:
                    dve.wait_ge(gathered[t], 16)
                else:
                    dve.wait_ge(S["gathered_rest"], 16 * (T - GATHERED_ALONE))
                norm_stats(0, 0, H[:, t, :], t)

            def a_norm(t):
                normalise(yA[:], H[:, t, :], 0, t).then_inc(src_ready[0], 1)

            def a_qkv(t):
                dve.wait_ge(S["qk0_psum"], t + 1)
                link(0, t, dve.tensor_tensor(xA[:], by4(psA[:, 1, :]), chunk_bias(qk0_bias, 4), ALU.add))
                dve.tensor_scalar(qz[:].rearrange("p a b n -> p (a b) n"), xA[:], 0.0, None,
                                  ALU.min).then_inc(S["xmin_ready"], 1)
                dve.wait_ge(S["v0_psum"], t + 1)
                values(voA, psA[:, 2, :], row["v0_bias"], "v0_ready")

            def a_elu(t):
                dve.wait_ge(S["exp_ready"], t + 1)
                link(0, t, dve.scalar_tensor_tensor(out=qkA[:], in0=xA[:], scalar=0.0,
                                                    in1=qz[:].rearrange("p a b n -> p (a b) n"),
                                                    op0=ALU.max, op1=ALU.add))
                for a in range(2):
                    link(0, t, dve.tensor_scalar(qz[:, :, a, :], qkA[:, 0:KD, :], FEAT_EPS, parity[:, a:a + 1],
                                                 ALU.add, ALU.mult))
                dve.tensor_scalar(qkA[:, KD:4, :], qkA[:, KD:4, :], FEAT_EPS, None,
                                  ALU.add).then_inc(S["qk0_ready"], 1)

            def a_mask(t):
                for b in range(4):
                    dve.wait_ge(S["scores_psum"], t * 4 + (b + 1))
                    dve.tensor_tensor(S_sb[:, b], by4(psA[:, b % 3, :]),
                                      causal_sb[:].unsqueeze(1).broadcast_to([P, 4, P]), ALU.mult
                                      ).then_inc(S["scores_masked"], 1)

            def a_mean(t):
                dve.wait_ge(S["heads0_psum"], t * 4 + 4)
                weighted_mean(0, t, psA[:, 1, :], denA, 4 * FEAT_EPS, tmpA, 1)

            def a_out(t):
                dve.wait_ge(S["out0_psum"], t + 1)
                link(0, t, dve.tensor_tensor(tmpA[:], psA[:, 0, 0:D], row["out0_bias"], ALU.add))
                norm_stats(1, 0, tmpA[:], t)

            def a_residual(t):
                link(0, t, normalise(tmpA[:], tmpA[:], 1, t))
                link(0, t, dve.tensor_tensor(tmpA[:], tmpA[:], row["gamma0"], ALU.mult))
                dve.wait_ge(S["preA_ready"], t + 1)
                link(0, t, dve.tensor_tensor(H[:, t, :], tmpA[:], preA[:], ALU.add))
                norm_stats(2, 0, H[:, t, :], t)

            def a_norm2(t):
                normalise(yA[:], H[:, t, :], 2, t).then_inc(src_ready[2], 1)

            def a_ffn(t):
                dve.wait_ge(S["ffn0_psum"], t + 1)
                link(0, t, dve.tensor_tensor(tmpA[:], psA[:, 1, 0:D], row["ffn0_scb"], ALU.mult))
                dve.wait_ge(S["preA2_ready"], t + 1)
                link(0, t, dve.tensor_tensor(H[:, t, :], tmpA[:], preA[:], ALU.add))

            def b_stats(t):
                begins(1)
                norm_stats(3, 1, H[:, t, :], t)

            def b_norm(t):
                normalise(yB[:], H[:, t, :], 3, t).then_inc(src_ready[3], 1)

            def b_qkv(t):
                dve.wait_ge(S["qk1_psum"], t + 1)
                dve.tensor_tensor(qkB[:], by4(psB[:, 1, :]), chunk_bias(qk1_bias, 4), ALU.add).then_inc(S["qk1_ready"], 1)
                dve.wait_ge(S["v1_psum"], t + 1)
                values(voB, psB[:, 2, :], row["v1_bias"], "v1_ready")

            def b_kmax(t):
                dve.wait_ge(S["diag_psum"], t + 1)
                dve.tensor_copy(flat(diag[:]), psB[:, 0, 0:2 * HEADS]).then_inc(S["diag_read"], 1)
                dve.wait_ge(S["xk_read"], t + 1)
                dve.tensor_reduce(kmax[:, 0, :], kf[:], AX.X, ALU.max).then_inc(S["kmax_ready"], 1)

            def b_q(t):
                xq = psB[:, 0:2, :].rearrange("p b (h m) -> p (b h) m", m=M)
                dve.wait_ge(S["xq_psum"], t + 1)
                link(1, t, dve.tensor_reduce(qmax[:, 0, :], xq, AX.X, ALU.max))
                link(1, t, dve.tensor_tensor(qmax[:, 1, :], qmax[:, 0, :], diag[:, 0, :], ALU.add))
                dve.tensor_tensor(qf[:], xq, by_head(qmax[:, 1, :], M), ALU.subtract).then_inc(S["qexp_in"], 1)

            def b_k(t):
                dve.wait_ge(S["kmax_all"], t + 1)
                link(1, t, dve.tensor_tensor(kmax[:, 2, :], kmax[:, 1, :], diag[:, 1, :], ALU.add))
                dve.tensor_tensor(kf[:], kf[:], by_head(kmax[:, 2, :], M), ALU.subtract).then_inc(S["kexp_in"], 1)

            def b_keps(t):
                dve.wait_ge(S["kexp_out"], t + 1)
                dve.tensor_scalar(kf[:], kf[:], EPS_K, None, ALU.add).then_inc(S["kfeat_ready"], 1)

            def b_ctx(t):
                dve.wait_ge(S["ctx_psum"], t * 4 + 4)
                pairs = psB[:, 2, 0:PAIRS * 2 * V1].rearrange("p (a v) -> p a v", a=PAIRS)
                for a in range(2):
                    dve.tensor_copy(ctxbd[M * a:M * a + M, :, V1 * a:V1 * a + V1],
                                    pairs[M * a:M * a + M, :, V1 * a:V1 * a + V1]).then_inc(S["ctx_ready"], 1)

            def b_mean(t):
                dve.wait_ge(S["heads1_psum"], t * 4 + 4)
                weighted_mean(1, t, psB[:, 2, :], denB, 0.0, tmpB, 4)

            def b_out(t):
                dve.wait_ge(S["out1_psum"], t + 1)
                dve.wait_ge(S["preB_ready"], t + 1)
                link(1, t, dve.tensor_tensor(tmpB[:], psB[:, 1, 0:D], preB[:], ALU.add))
                norm_stats(4, 1, tmpB[:], t)

            def b_x(t):
                link(1, t, normalise(tmpB[:], tmpB[:], 4, t))
                link(1, t, dve.tensor_tensor(tmpB[:], tmpB[:], row["g2"], ALU.mult))
                dve.tensor_tensor(x1[:], tmpB[:], row["be2"], ALU.add).then_inc(S["x1_ready"], 1)

            def c_ff(t):
                begins(2)
                dve.wait_ge(S["ff2_psum"], t * 2 + 2)
                dve.wait_ge(S["preC_ready"], t + 1)
                link(2, t, dve.tensor_tensor(tmpC[:], psC[:, 1, 0:D], preC[:], ALU.add))
                norm_stats(5, 2, tmpC[:], t)

            def c_residual(t):
                link(2, t, normalise(tmpC[:], tmpC[:], 5, t))
                link(2, t, dve.tensor_tensor(tmpC[:], tmpC[:], row["g3"], ALU.mult))
                dve.wait_ge(S["hC_ahead"], t + 1)
                link(2, t, dve.tensor_tensor(H[:, t, :], tmpC[:], H[:, t, :], ALU.add))
                norm_stats(6, 2, H[:, t, :], t)

            def c_norm(t):
                normalise(yC[:], H[:, t, :], 6, t).then_inc(src_ready[6], 1)

            def c_logits(t):
                dve.wait_ge(S["logit_psum"], t + 1)
                link(2, t, dve.tensor_copy(logits[:, t, :], psC[:, 1, 0:E]))
                dve.tensor_reduce(top[:, 0:1], psC[:, 1, 0:E], AX.X, ALU.max).then_inc(S["logit_read"], 1)

            def c_hidden(t):
                dve.wait_ge(S["tanh_top"], t + 1)
                link(2, t, dve.tensor_scalar(top[:, 2:3], top[:, 1:2], 0.5, 0.5, ALU.mult, ALU.add))
                link(2, t, dve.tensor_scalar(Y[:, t, :], yC[:], top[:, 2:3], None, ALU.mult))
                dve.wait_ge(S["tanh_gate"], t + 1)
                link(2, t, dve.scalar_tensor_tensor(out=gC[:], in0=tC[:], scalar=1.0, in1=psC[:, 0, :],
                                                    op0=ALU.add, op1=ALU.mult))
                dve.wait_ge(S["up_psum"], t + 1)
                dve.scalar_tensor_tensor(out=flat(hT[:]), in0=gC[:], scalar=0.5, in1=psC[:, 1, :],
                                         op0=ALU.mult, op1=ALU.mult).then_inc(S["hT_ready"], 1)

            def c_down(t):
                dve.wait_ge(S["down_psum"], t + 1)
                link(2, t, dve.tensor_tensor(H[:, t, :], psC[:, 0, 0:D], H[:, t, :], ALU.add))
                dve.sem_inc(S["tile_done"], 1)

            dve.wait_ge(S["vectors_loaded"], 16)
            dve.tensor_scalar(row["ffn0_scb"], row["ffn0_scb"], 1.0 / 127.0, None, ALU.mult).then_inc(S["unused2"], 1)
            dve.wait_ge(S["unused2"], 1)
            dve.wait_ge(S["small_loaded"], 16 * 2)
            dve.wait_ge(S["proj_loaded"], 16 * 8)
            dve.tensor_scalar(proj_sb[:], proj_sb[:], float(DH) ** -0.25, None, ALU.mult).then_inc(S["proj_scaled"], 1)
            dve.wait_ge(S["consts_ready"], 4)
            run_steps(dve, [
                (B, b_stats), (A, a_stats), (B, b_norm), (A, a_norm), (B, b_qkv), (A, a_qkv), (A, a_elu), (B, b_kmax),
                (A, a_mask), (B, b_q), (B, b_k), (C, c_ff), (B, b_keps), (A, a_mean), (C, c_residual), (B, b_ctx),
                (C, c_norm), (A, a_out), (B, b_mean), (C, c_logits), (A, a_residual), (C, c_hidden), (B, b_out),
                (A, a_norm2), (B, b_x), (C, c_down), (A, a_ffn),
            ])
            steps = [0]

            def then(ins):
                steps[0] += 1
                ins.then_inc(S["routing_step"], 1)
                dve.wait_ge(S["routing_step"], steps[0])

            dve.wait_ge(S["tile_done"], T)
            rev = cols_sb[:, 10 + KF:10 + KF + E]
            full = cols_sb[:, 10 + KF + E:10 + KF + E + T]
            number = cols_sb[:, 10 + KF + E + T:10 + KF + E + T + SORTED_TILES]

            def over_t(v):
                return v.unsqueeze(1).broadcast_to([P, T, E])

            def over_e(v):
                return v.unsqueeze(2).broadcast_to([P, T, E])

            then(dve.tensor_reduce(rt[:, 0:T], logits[:], AX.X, ALU.max))
            then(dve.tensor_tensor(ra, logits[:], over_e(rt[:, 0:T]), ALU.is_equal))
            then(dve.tensor_tensor(rb, ra, over_t(rev), ALU.mult))
            then(dve.tensor_reduce(rt[:, 0:T], rb, AX.X, ALU.max))
            then(dve.tensor_tensor(onehot, over_t(rev), over_e(rt[:, 0:T]), ALU.is_equal))
            dve.sem_inc(S["onehot_ready"], 1)
            dve.wait_ge(S["count_psum"], 1)
            then(dve.tensor_copy(counts, psB[:, 1, 0:T * E].rearrange("p (t e) -> p t e", t=T)))
            then(dve.tensor_copy(ra, counts))
            src, dst, d = ra, rb, 1
            while d < T:
                then(dve.tensor_copy(dst[:, 0:d, :], src[:, 0:d, :]))
                then(dve.tensor_tensor(dst[:, d:T, :], src[:, d:T, :], src[:, 0:T - d, :], ALU.add))
                src, dst, d = dst, src, 2 * d
            total = src[:, T - 1, :]
            need = flatS[:, 1024:1024 + E * T].rearrange("p (e k) -> p e k", e=E)
            then(dve.tensor_tensor(need, total.unsqueeze(2).broadcast_to([P, E, T]),
                                   full.unsqueeze(1).broadcast_to([P, E, T]), ALU.is_gt))
            then(dve.tensor_reduce(rt[:, 0:E], need, AX.X, ALU.add))
            then(dve.tensor_copy(rt[:, E:2 * E], rt[:, 0:E]))
            at, to, d = 1, 2, 1
            while d < E:
                then(dve.tensor_copy(rt[:, to * E:to * E + d], rt[:, at * E:at * E + d]))
                then(dve.tensor_tensor(rt[:, to * E + d:(to + 1) * E], rt[:, at * E + d:(at + 1) * E],
                                       rt[:, at * E:(at + 1) * E - d], ALU.add))
                at, to, d = to, at, 2 * d
            ends = rt[:, at * E:(at + 1) * E]
            then(dve.tensor_tensor(rt[:, 3 * E:4 * E], ends, rt[:, 0:E], ALU.subtract))
            before_tile = flatS[:, 1280:1280 + SORTED_TILES * E].rearrange("p (j e) -> p j e", e=E)
            then(dve.tensor_tensor(before_tile, ends.unsqueeze(1).broadcast_to([P, SORTED_TILES, E]),
                                   number.unsqueeze(2).broadcast_to([P, SORTED_TILES, E]), ALU.is_le))
            then(dve.tensor_reduce(rt[:, 4 * E:4 * E + SORTED_TILES], before_tile, AX.X, ALU.add))
            then(dve.tensor_scalar(tile_expert, rt[:, 4 * E:4 * E + SORTED_TILES], float(E - 1), None, ALU.min))
            then(dve.tensor_scalar(rt[:, 3 * E:4 * E], rt[:, 3 * E:4 * E], float(P), None, ALU.mult))
            then(dve.tensor_tensor(dst, src, counts, ALU.subtract))
            then(dve.tensor_tensor(src, dst, psB[:, 0, 0:T * E].rearrange("p (t e) -> p t e", t=T), ALU.add))
            then(dve.tensor_tensor(dst, src, over_t(rt[:, 3 * E:4 * E]), ALU.add))
            then(dve.tensor_tensor(src, dst, onehot, ALU.mult))
            then(dve.tensor_reduce(rt[:, 0:T], src, AX.X, ALU.add))
            then(dve.tensor_copy(slot_u[:], rt[:, 0:T]))
            dve.sem_inc(S["slots_ready"], 1)

            with dve.Fori(0, SORTED_TILES // MOE_SLOTS) as i:
                for s in range(MOE_SLOTS):
                    j = i * MOE_SLOTS + s
                    dve.wait_ge(S["tanh_eg"], j + 1)
                    dve.scalar_tensor_tensor(out=eg2[s], in0=eg1[s], scalar=1.0, in1=banks_of[s][1],
                                             op0=ALU.add, op1=ALU.mult).then_inc(S["eg_ready"], 1)
                    dve.wait_ge(S["eg_ready"], j + 1)
                    dve.wait_ge(S["eu_psum"], j + 1)
                    dve.scalar_tensor_tensor(out=flat(eh[s]), in0=eg2[s], scalar=0.5, in1=banks_of[s][2],
                                             op0=ALU.mult, op1=ALU.mult).then_inc(S["eh_ready"], 1)
                for s in range(MOE_SLOTS):
                    dve.wait_ge(S["ey_free"], i * MOE_SLOTS + s + 1)
                    dve.wait_ge(S["ey_psum"], i * MOE_SLOTS + s + 1)
                    dve.tensor_copy(ey[s], banks_of[s][3][:, 0:D]).then_inc(S["ey_ready"], 1)
            for q in range(4):
                n = T // 4
                dve.wait_ge(fetched[q], 16 * n)
                dve.tensor_tensor(H[:, q * n:(q + 1) * n, :], H[:, q * n:(q + 1) * n, :], Y[:, q * n:(q + 1) * n, :],
                                  ALU.add).then_inc(S["added"], 1)

        @block.tensor
        def _(pe):
            def matmul(o, a, b, start, stop):
                return pe.matmul(o, a, b, start=start, stop=stop)

            def transposed(k, dst, src):
                def stage(t):
                    pe.wait_ge(S["x1_ready"] if k == 5 else src_ready[k], t + 1)
                    if k == 5:
                        pe.wait_ge(S["tile_done"], t)
                    for c in range(KD):
                        ins = pe.transpose(dst[:, c * P:(c + 1) * P], src[:, c * P:(c + 1) * P], id_sb[:])
                    ins.then_inc(srcT_psum[k], 1)
                return stage

            def by_token(o, a, b, chunks):
                for c in range(chunks):
                    ins = matmul(o, a[:, c, :], b[:, c, :], c == 0, c == chunks - 1)
                return ins

            def by_channel(bank, yT, w, blocks):
                for n, m in enumerate(blocks):
                    for c in range(KD):
                        ins = matmul(bank[:, n * P:(n + 1) * P], w[:, c, m * P:(m + 1) * P], yT[:, c, :],
                                     c == 0, c == KD - 1)
                return ins

            def a_qkv(t):
                pe.wait_ge(srcT_ready[0], t + 1)
                by_channel(psA[:, 1, :], yTA, qk0_sb, range(4)).then_inc(S["qk0_psum"], 1)
                by_token(psA[:, 2, 0:D], yTA, v0_sb, KD).then_inc(S["v0_psum"], 1)

            def a_scores(b):
                def stage(t):
                    if b == 0:
                        pe.wait_ge(S["qk0_ready"], t + 1)
                        pe.wait_ge(S["v0_ready"], t + 1)
                    if b == 3:
                        pe.wait_ge(S["scores_masked"], t * 4 + 1)
                    rows_of = slice(32 * b, 32 * b + 32)
                    for half in range(2):
                        ins = matmul(psA[:, b % 3, half * 256:half * 256 + 256], qkA[rows_of, KD + half, :],
                                     qz[rows_of, half].rearrange("p a n -> p (a n)"), True, True)
                    ins.then_inc(S["scores_psum"], 1)
                return stage

            def a_heads(b):
                def stage(t):
                    pe.wait_ge(S["scores_masked"], t * 4 + max(b + 1, 2))
                    for half in range(2):
                        for a in range(2):
                            h = 2 * (4 * half + b) + a
                            ins = matmul(heads(psA[:, 1, :])[:, h, :], S_sb[:, b, 2 * half + a, :], voA[:, h, :],
                                         True, True)
                    ins.then_inc(S["heads0_psum"], 1)
                return stage

            def a_out(t):
                pe.wait_ge(srcT_ready[1], t + 1)
                by_token(psA[:, 0, 0:D], yTA, out0_sb, KD).then_inc(S["out0_psum"], 1)

            def a_ffn(t):
                pe.wait_ge(srcT_ready[2], t + 1)
                by_token(psA[:, 1, 0:D], yTA, cb_sb, KD).then_inc(S["ffn0_psum"], 1)

            def b_qkv(t):
                pe.wait_ge(srcT_ready[3], t + 1)
                by_channel(psB[:, 1, :], yTB, qk1_sb, range(4)).then_inc(S["qk1_psum"], 1)
                by_token(psB[:, 2, 0:D], yTB, v1w_sb, KD).then_inc(S["v1_psum"], 1)

            def b_diag(t):
                pe.wait_ge(S["square_ready"], t + 1)
                for c in range(4):
                    ins = matmul(psB[:, 0, 8 * c:8 * c + 8], sqB[:, c, :], hsum_sb[:], True, True)
                ins.then_inc(S["diag_psum"], 1)

            def b_k(t):
                pe.wait_ge(S["v1_ready"], t + 1)
                for c in range(KD):
                    ins = matmul(psB[:, 1 + c, :], qkB[:, KD + c, :], proj_sb[:], True, True)
                ins.then_inc(S["xk_psum"], 1)

            def b_q(t):
                pe.wait_ge(S["diag_read"], t + 1)
                pe.wait_ge(S["xk_read"], t + 1)
                for c in range(KD):
                    ins = matmul(psB[:, c, :], qkB[:, c, :], proj_sb[:], True, True)
                ins.then_inc(S["xq_psum"], 1)

            def b_qT(t):
                pe.wait_ge(S["qfeat_ready"], t + 1)
                for pair in range(PAIRS):
                    ins = pe.transpose(psB[:, pair // 4, pair % 4 * P:pair % 4 * P + P],
                                       flat(qf[:])[:, pair * P:(pair + 1) * P], id_sb[:])
                ins.then_inc(S["qT_psum"], 1)

            def b_ctx(quarter):
                def stage(t):
                    if quarter == 0:
                        pe.wait_ge(S["kfeat_ready"], t + 1)
                    for pair in range(2 * quarter, 2 * quarter + 2):
                        ins = matmul(psB[:, 2, pair * 2 * V1:(pair + 1) * 2 * V1],
                                     flat(kf[:])[:, pair * P:(pair + 1) * P],
                                     flat(voB[:, 2 * pair:2 * pair + 2, :]), True, True)
                    ins.then_inc(S["ctx_psum"], 1)
                return stage

            def b_heads(quarter):
                def stage(t):
                    if quarter == 0:
                        pe.wait_ge(S["ctx_ready"], t * 2 + 2)
                        pe.wait_ge(S["qT_ready"], t + 1)
                    for pair in range(2 * quarter, 2 * quarter + 2):
                        ins = matmul(psB[:, 2, pair * 2 * V1:(pair + 1) * 2 * V1], qfT[:, pair, :],
                                     ctxbd[:, pair, :], True, True)
                    ins.then_inc(S["heads1_psum"], 1)
                return stage

            def b_out(t):
                pe.wait_ge(srcT_ready[4], t + 1)
                by_token(psB[:, 1, 0:D], yTB, out1_sb, KD).then_inc(S["out1_psum"], 1)

            def c_ff1(half):
                def stage(t):
                    pe.wait_ge(srcT_ready[5], t + 1)
                    by_channel(psC[:, 1 - half, :], yTC, ff1_sb, range(4 * half, 4 * half + 4)
                               ).then_inc(S["ff1_psum"], 1)
                return stage

            def c_ff2(half):
                def stage(t):
                    pe.wait_ge(S["ff_ready"], t * KF + KF)
                    for c in range(KF // 2 * half, KF // 2 * (half + 1)):
                        ins = matmul(psC[:, 1, 0:D], ffT[:, c, :], ff2_sb[:, c, :], c == 0, c == KF - 1)
                    ins.then_inc(S["ff2_psum"], 1)
                return stage

            def c_gate(t):
                pe.wait_ge(srcT_ready[6], t + 1)
                by_token(psC[:, 1, 0:E], yTC, router_sb, KD).then_inc(S["logit_psum"], 1)
                by_channel(psC[:, 0, :], yTC, sg_sb, range(KE)).then_inc(S["gate_psum"], 1)

            def c_up(t):
                pe.wait_ge(S["logit_read"], t + 1)
                by_channel(psC[:, 1, :], yTC, su_sb, range(KE)).then_inc(S["up_psum"], 1)

            def c_down(t):
                pe.wait_ge(S["hT_ready"], t + 1)
                by_token(psC[:, 0, 0:D], hT, sd_sb, KE).then_inc(S["down_psum"], 1)

            def once(stage, name, value):
                def first(t):
                    if not isinstance(t, int) or t == 0:
                        pe.wait_ge(S[name], value)
                    stage(t)
                return first

            pe.wait_ge(S["small_loaded"], 16 * 2)
            run_steps(pe, [
                (C, transposed(5, psC[:, 0, :], x1)), (C, once(c_ff1(0), "last_loaded", 16 * 7)), (C, c_ff1(1)),
                (B, transposed(3, psB[:, 0, :], yB)), (A, transposed(0, psA[:, 0, :], yA)), (B, b_qkv),
                (A, once(a_qkv, "block0_loaded", 16 * 4)), (B, b_diag), (B, once(b_k, "proj_scaled", 1)),
                (A, a_scores(0)), (A, a_scores(1)), (B, b_q), (A, a_scores(2)), (A, a_scores(3)), (A, a_heads(0)),
                (C, c_ff2(0)), (A, a_heads(1)), (C, c_ff2(1)), (A, a_heads(2)), (A, a_heads(3)), (B, b_qT),
                (B, b_ctx(0)), (A, transposed(1, psA[:, 2, :], tmpA)), (B, b_ctx(1)), (B, b_ctx(2)), (B, b_ctx(3)),
                (A, a_out), (B, b_heads(0)), (B, b_heads(1)), (C, transposed(6, psC[:, 0, :], yC)), (B, b_heads(2)),
                (B, b_heads(3)), (C, c_gate), (B, transposed(4, psB[:, 0, :], tmpB)), (C, c_up), (B, b_out),
                (C, c_down), (A, transposed(2, psA[:, 0, :], yA)), (A, once(a_ffn, "middle_loaded", 16 * 5)),
            ])
            pe.wait_ge(S["onehot_ready"], 1)
            chosen = onehot.rearrange("p t e -> p (t e)")
            matmul(psB[:, 0, 0:T * E], before_sb[:], chosen, True, True)
            matmul(psB[:, 1, 0:T * E], ones_sb[:], chosen, True, True).then_inc(S["count_psum"], 1)
            pe.wait_ge(S["slots_ready"], 1)
            pe.wait_ge(S["experts_loaded"], 16 * RESIDENT)
            pe.wait_ge(S["late_loaded"], 16 * (E - RESIDENT))
            with pe.Fori(0, SORTED_TILES // MOE_SLOTS) as i:
                for s in range(MOE_SLOTS):
                    pe.wait_ge(x_loaded[s], i * 16 + 16)
                    for c in range(KD):
                        ins = pe.transpose(banks_of[s][0][:, c * P:(c + 1) * P], xm[s][:, c * P:(c + 1) * P], id_sb[:])
                    ins.then_inc(S["xT_psum"], 1)
                expert = [pe.value_load(tile_expert[0:1, bass.ds(i * MOE_SLOTS + s, 1)], min_val=0, max_val=E - 1)
                          for s in range(MOE_SLOTS)]
                for s in range(MOE_SLOTS):
                    pe.wait_ge(S["xT_ready"], i * MOE_SLOTS + s + 1)
                    for b, at, done in ((1, GATE, "eg_psum"), (2, UP, "eu_psum")):
                        for c in range(KD):
                            ins = matmul(banks_of[s][b], xT[s][:, c, :], we[:, bass.ds(expert[s] * EXPERT + (at + c * F), F)],
                                         c == 0, c == KD - 1)
                        ins.then_inc(S[done], 1)
                for s in range(MOE_SLOTS):
                    pe.wait_ge(S["eh_ready"], i * MOE_SLOTS + s + 1)
                    for c in range(KE):
                        ins = pe.transpose(banks_of[s][3][:, c * P:(c + 1) * P], eh[s][:, c, :], id_sb[:])
                    ins.then_inc(S["ehT_psum"], 1)
                for s in range(MOE_SLOTS):
                    pe.wait_ge(S["ehT_ready"], i * MOE_SLOTS + s + 1)
                    for c in range(KE):
                        ins = matmul(banks_of[s][3][:, 0:D], ehT[s][:, c, :],
                                     we[:, bass.ds(expert[s] * EXPERT + (DOWN + c * D), D)], c == 0, c == KE - 1)
                    ins.then_inc(S["ey_psum"], 1)

    return nc


def kernel(**inputs):
    import numpy as np
    import concourse.bacc as bacc
    from concourse.bass_utils import run_bass_kernel_spmd

    a = {k: np.asarray(v) for k, v in inputs.items()}

    def chunks(w):
        return np.ascontiguousarray(w.reshape(-1, 128, w.shape[1]).transpose(1, 0, 2))

    def column(v):
        return v.reshape(-1, 128).T

    D = a["L0_tok_weight"].shape[1]
    E = a["L1_ffn_router_w"].shape[0]
    T = a["x"].shape[0]
    qkv0, b0 = a["L0_attn_Wqkv"], a["L0_attn_bqkv"]
    f4 = np.float32
    part = np.arange(128)
    parity = np.stack([part // 16 % 2 == 0, part // 16 % 2 == 1], 1).astype(f4)
    counts = np.concatenate([E - np.arange(E), 128 * np.arange(T), np.arange(T + E)]).astype(f4)
    experts = np.concatenate([
        a["L1_ffn_expert_gate"].reshape(E, D // 128, 128, -1).transpose(0, 2, 1, 3).reshape(E, 128, -1),
        a["L1_ffn_expert_up"].reshape(E, D // 128, 128, -1).transpose(0, 2, 1, 3).reshape(E, 128, -1),
        a["L1_ffn_expert_down"].reshape(E, -1, 128, D).transpose(0, 2, 1, 3).reshape(E, 128, -1)], axis=2)
    arrays = {
        "idx": np.ascontiguousarray(a["x"].T.view(np.uint32)),
        "table": a["L0_tok_weight"],
        "w_qk0": chunks(qkv0[0:2 * D].T), "w_v0": chunks(qkv0[2 * D:].T), "w_out0": chunks(a["L0_attn_Wout"].T),
        "cb": chunks(a["L0_ffn_CB"].T),
        "w_qk1": chunks(np.concatenate([a["L1_attn_Wq"], a["L1_attn_Wk"]]).T),
        "w_v1": chunks(a["L1_attn_Wv"].T), "w_out1": chunks(a["L1_attn_Wo"].T),
        "proj": np.ascontiguousarray(a["L1_attn_proj"].T),
        "w_ff1": chunks(a["L1_attn_W1"].T), "w_ff2": chunks(a["L1_attn_W2"].T),
        "w_router": chunks(a["L1_ffn_router_w"].T),
        "w_shared_gate": chunks(a["L1_ffn_shared_gate"]), "w_shared_up": chunks(a["L1_ffn_shared_up"]),
        "w_shared_down": chunks(a["L1_ffn_shared_down"]),
        "w_experts": experts,
        "rows": np.stack([b0[2 * D:], a["L0_attn_bout"], a["L0_attn_gamma"], a["L0_attn_beta"], a["L0_ffn_SCB"],
                          a["L0_ffn_bias"], a["L1_attn_bv"], a["L1_attn_bo"], a["L1_attn_g2"], a["L1_attn_be2"],
                          a["L1_attn_b2"], a["L1_attn_g3"], a["L1_attn_be3"]]),
        "cols": np.concatenate([column(b0[0:2 * D]), column(a["L1_attn_bq"]), column(a["L1_attn_bk"]),
                                column(a["L1_attn_b1"]), parity, np.broadcast_to(counts, (128, counts.size))], axis=1),
        "ident": np.eye(128, dtype=f4),
        "causal": (part[:, None] <= part[None, :]).astype(f4),
        "head_sum": 0.125 * (part[:, None] // 16 == np.arange(8)[None, :]).astype(f4),
        "before": (part[:, None] < part[None, :]).astype(f4),
    }
    nc = bacc.Bacc("TRN2", target_bir_lowering=False, num_devices=1)
    arrays = {k: np.ascontiguousarray(v) for k, v in arrays.items()}
    args = [nc.dram_tensor(k, v.shape, mybir.dt.from_np(v.dtype), kind="ExternalInput").ap() for k, v in arrays.items()]
    out = nc.dram_tensor("out", (T, 128, D), F32, kind="ExternalOutput").ap()
    bass_lm_tower(nc, *args, out)
    r = run_bass_kernel_spmd(nc, [arrays], core_ids=[0])
    return r.results[0]["out"]
```

```python
from contextlib import ExitStack

import concourse.bass as bass
from concourse import mybir

ALU = mybir.AluOpType
ACT = mybir.ActivationFunctionType
AX = mybir.AxisListType
F32 = mybir.dt.float32
F16 = mybir.dt.float16
F32R = mybir.dt.float32r
U32 = mybir.dt.uint32
I32 = mybir.dt.int32
MAX = bass.bass_isa.ReduceOp.max

P = 128
MOE_SLOTS = 2
PIECES = 3
LN, TR = 7, 7
A, B, C = range(PIECES)
GATHERED_ALONE = 3
LINKS = [15, 10, 20]
LN_EPS = 1e-5
FEAT_EPS = 1e-4
EPS_K = 1e-4

ROWS = ["v0_bias", "out0_bias", "gamma0", "beta0", "ffn0_scb", "ffn0_bias",
        "v1_bias", "out1_bias", "g2", "be2", "b2", "g3", "be3"]


def bass_lm_tower(nc, idx, table, w_qk0, w_v0, w_out0, cb, w_qk1, w_v1, w_out1, proj, w_ff1, w_ff2,
                  w_router, w_shared_gate, w_shared_up, w_shared_down, w_experts, rows, cols, ident, causal,
                  head_sum, before, out):
    D = table.shape[1]
    T = idx.shape[1]
    KD = D // P
    HEADS, DH = 16, D // 16
    PAIRS = HEADS // 2
    M = proj.shape[1]
    FF1 = w_ff1.shape[2]
    KF = FF1 // P
    F = w_shared_gate.shape[2]
    KE = F // P
    E = w_router.shape[2]
    V1 = DH + 1
    EXPERT = w_experts.shape[2]
    SORTED_TILES = T + E - 1
    ROUNDS = -(-SORTED_TILES // MOE_SLOTS)
    SPAN = T + 1
    ROW = 2 * D + 1
    NOWHERE = 1 << 14
    GATE, UP, DOWN = 0, KD * F, 2 * KD * F
    RESIDENT = 4
    with ExitStack() as ctx:
        def sb(name, shape, dt=F32):
            return ctx.enter_context(nc.sbuf_tensor(name, shape, dt))

        def sem(name):
            return ctx.enter_context(nc.semaphore(name))

        we = sb("we", [P, E * EXPERT])
        H = sb("H", [P, T, D])
        send = sb("send", [P, ROW])
        pads = sb("pads", [P, ROW])
        home = [sb(f"home{s}", [P, D + 1]) for s in range(MOE_SLOTS)]
        idx_sb = sb("idx_sb", [P, T], U32)
        id_sb = sb("id_sb", [P, P])
        before_sb = sb("before_sb", [P, P])
        ones_sb = sb("ones_sb", [P, P], F16)
        before16 = sb("before16", [P, P], F16)
        pow_half = sb("pow_half", [P, 1])
        ln_eps = sb("ln_eps", [P, 1])
        cols_sb = sb("cols_sb", [P, cols.shape[1]])
        spare = [RESIDENT * EXPERT, E * EXPERT]

        def overlaid(k, n):
            at = spare[0]
            spare[0] += k * n
            assert spare[0] <= spare[1]
            return we[:, at:at + k * n].rearrange("p (k n) -> p k n", k=k)

        qk0_sb, v0_sb, out0_sb, cb_sb = overlaid(KD, 2 * D), overlaid(KD, D), overlaid(KD, D), overlaid(KD, D)
        qk1_sb, v1w_sb, out1_sb = overlaid(KD, 2 * D), overlaid(KD, D), overlaid(KD, D)
        freed_by_b = spare[0] // EXPERT
        ff1_sb, ff2_sb = overlaid(KD, FF1), overlaid(KF, D)
        freed_by_ff = E - 1
        assert spare[0] <= freed_by_ff * EXPERT
        spare[0] = freed_by_ff * EXPERT
        sg_sb, su_sb, sd_sb = overlaid(KD, F), overlaid(KD, F), overlaid(KE, D)
        router_sb = sb("router_sb", [P, KD, E])
        proj_sb = sb("proj_sb", [P, 8 * M])
        rows_sb = sb("rows_sb", [P, len(ROWS), D])
        causal_sb = sb("causal_sb", [P, P])
        hsum_sb = sb("hsum_sb", [P, 8])
        row = {n: rows_sb[:, i, :] for i, n in enumerate(ROWS)}
        at = [0]

        def columns(n):
            at[0] += n
            return cols_sb[:, at[0] - n:at[0]]

        qk0_bias, qk1_bias, b1_col, parity = columns(4), columns(4), columns(KF), columns(2)
        rev = columns(E)
        full = columns(T)
        number = columns(SORTED_TILES)
        start_row = columns(E)
        partition = columns(1)
        yA, tmpA, preA = sb("yA", [P, D]), sb("tmpA", [P, D]), sb("preA", [P, D])
        yTA = sb("yTA", [P, KD, P])
        qkA = sb("qkA", [P, 4, P])
        xA = sb("xA", [P, 4, P])
        qz = sb("qz", [P, KD, 2, P])
        voA = sb("voA", [P, HEADS, V1])
        S_sb = sb("S_sb", [P, 4, 4, P])
        yB, tmpB, preB = sb("yB", [P, D]), sb("tmpB", [P, D]), sb("preB", [P, D])
        yTB = sb("yTB", [P, KD, P])
        qkB = sb("qkB", [P, 4, P])
        sqB = sb("sqB", [P, 4, P])
        qkR = sb("qkR", [P, 2, 4, P], F32R)
        projR = sb("projR", [P, 2, 8 * M], F32R)
        voB = sb("voB", [P, HEADS, V1])
        kf = sb("kf", [P, HEADS, M])
        qf = sb("qf", [P, HEADS, M])
        qfT = sb("qfT", [P, PAIRS, P])
        ctxbd = sb("ctxbd", [P, PAIRS, 2 * V1])
        x1, yC, tmpC, preC = sb("x1", [P, D]), sb("yC", [P, D]), sb("tmpC", [P, D]), sb("preC", [P, D])
        yTC = sb("yTC", [P, KD, P])
        ffT = sb("ffT", [P, KF, P])
        gC = sb("gC", [P, F])
        tC = sb("tC", [P, F])
        hT = sb("hT", [P, KE, P])
        stats = sb("stats", [P, 7, 6])
        mv = sb("mv", [P, 7, 2])
        rstd = sb("rstd", [P, 7, 2])
        denA = sb("denA", [P, 2, HEADS])
        denB = sb("denB", [P, 2, HEADS])
        diag = sb("diag", [P, 2, HEADS])
        kmax = sb("kmax", [P, 3, HEADS])
        qmax = sb("qmax", [P, 2, HEADS])
        top = sb("top", [P, 4])
        psA = ctx.enter_context(nc.psum_tensor("psA", [P, 3, 512], F32))
        psB = ctx.enter_context(nc.psum_tensor("psB", [P, 3, 512], F32))
        psC = ctx.enter_context(nc.psum_tensor("psC", [P, 2, 512], F32))
        lg = sb("lg", [P, E])
        mark = sb("mark", [P, E])
        onehot = sb("onehot", [P, E], F16)
        base = sb("base", [P, E])
        rank = sb("rank", [P, 2, E])
        token = sb("token", [P, 1])
        slot = sb("slot", [P, 1])
        slot_u = sb("slot_u", [P, 1], U32)
        pad_slots = sb("pad_slots", [P, E], U32)
        rt = sb("rt", [P, 6 * E])
        flatS = S_sb[:].rearrange("p b a n -> p (b a n)")
        tile_expert = sb("tile_expert", [P, SORTED_TILES], I32)[:]
        tile_row = sb("tile_row", [P, SORTED_TILES], I32)[:]
        sorted_dram = nc.dram_tensor("sorted_rows", [(E * SPAN + 1) * P, ROW], F32, kind="Internal").ap()

        names = """idx_loaded small_loaded vectors_loaded zero_ready consts_ready gathered_rest
        qkv0_loaded out0_loaded middle_loaded last_loaded proj_loaded proj_scaled proj_high proj_split
        before_ready qk_high qk_split
        experts_loaded late_loaded
        qk0_psum v0_psum xmin_ready exp_ready qk0_ready v0_ready scores_psum scores_masked heads0_psum
        out0_psum preA_ready
        ffn0_psum preA2_ready qk1_psum v1_psum qk1_ready v1_ready square_ready diag_psum diag_read
        xk_psum xk_read kmax_ready kmax_all kexp_in kexp_out kfeat_ready xq_psum qexp_in qfeat_ready
        qT_psum qT_ready ctx_psum ctx_ready heads1_psum preB_ready out1_psum
        x1_ready preC_ready hC_ahead ff1_psum ff_ready ff2_psum
        logit_psum logit_read tanh_top gate_psum up_psum tanh_gate hT_ready down_psum tile_done
        onehot_ready count_psum slot_ready scattered pads_ready pads_known pads_stored
        pad_tile_stored table_ready xT_psum xT_ready eg_psum eu_psum
        tanh_eg eh_ready ehT_psum ehT_ready ey_psum ey_ready eg_ready
        table_step prepared unused""".split()
        S = {n: sem(n) for n in names}
        var_ready = [sem(f"var{k}_ready") for k in range(LN)]
        rstd_ready = [sem(f"rstd{k}_ready") for k in range(LN)]
        src_ready = [sem(f"src{k}_ready") for k in range(TR)]
        srcT_psum = [sem(f"src{k}T_psum") for k in range(TR)]
        srcT_ready = [sem(f"src{k}T_ready") for k in range(TR)]
        dve_step = [sem(f"dve_step_{x}") for x in "ABC"]
        gathered = [sem(f"gathered{t}") for t in range(GATHERED_ALONE)]
        x_loaded = [sem(f"x_loaded{s}") for s in range(MOE_SLOTS)]
        home_loaded = [sem(f"home_loaded{s}") for s in range(MOE_SLOTS)]
        home_stored = [sem(f"home_stored{s}") for s in range(MOE_SLOTS)]

        xm = [yA[:], yB[:]]
        xT = [yTA[:], yTB[:]]
        eg1 = [kf[:].rearrange("p h m -> p (h m)")[:, 0:F], qf[:].rearrange("p h m -> p (h m)")[:, 0:F]]
        eg2 = [kf[:].rearrange("p h m -> p (h m)")[:, F:2 * F], qf[:].rearrange("p h m -> p (h m)")[:, F:2 * F]]
        eh = [xA[:], sqB[:]]
        ehT = [qkA[:], qkB[:]]
        ey = [tmpA[:], tmpB[:]]
        banks_of = [[psA[:, 0, :], psA[:, 1, :], psA[:, 2, :], psC[:, 0, :]],
                    [psB[:, 0, :], psB[:, 1, :], psB[:, 2, :], psC[:, 1, :]]]

        def flat(v):
            return v.rearrange("p a n -> p (a n)")

        def by4(v):
            return v.rearrange("p (a n) -> p a n", a=4)

        def heads(b):
            return b[:, 0:HEADS * V1].rearrange("p (h v) -> p h v", h=HEADS)

        def chunk_bias(col, n):
            return col.unsqueeze(2).broadcast_to([P, n, P])

        def by_head(v, n):
            return v.unsqueeze(2).broadcast_to([P, HEADS, n])

        def run_steps(engine, order):
            def step(u, active):
                for p, stage in order:
                    if p in active:
                        stage(u - p)

            for u in range(PIECES - 1):
                step(u, range(u + 1))
            with engine.Fori(PIECES - 1, T) as u:
                step(u, range(PIECES))
            for u in range(T, T + PIECES - 1):
                step(u, range(u - T + 1, PIECES))

        def tiles_of(i):
            of_round = [(s, i * MOE_SLOTS + s) for s in range(MOE_SLOTS)]
            return [(s, j) for s, j in of_round if j < SORTED_TILES] if isinstance(i, int) else of_round

        block = ctx.enter_context(nc.Block())

        @block.sync
        def _(sp):
            sp.dma_start(idx_sb[:], idx).then_inc(S["idx_loaded"], 16)
            for dst, src in ((id_sb[:], ident), (cols_sb[:], cols)):
                sp.dma_start(dst, src).then_inc(S["small_loaded"], 16)
            for dst, src in ((qk0_sb, w_qk0), (v0_sb, w_v0)):
                sp.dma_start(dst, src).then_inc(S["qkv0_loaded"], 16)
            sp.wait_ge(gathered[0], 16)
            sp.dma_start(rows_sb[:], rows.partition_broadcast(P)).then_inc(S["vectors_loaded"], 16)
            sp.dma_start(causal_sb[:], causal).then_inc(S["out0_loaded"], 16)
            sp.dma_start(out0_sb, w_out0).then_inc(S["out0_loaded"], 16)
            sp.wait_ge(S["zero_ready"], 3)
            for h in range(8):
                sp.dma_start(proj_sb[DH * h:DH * h + DH, M * h:M * h + M], proj).then_inc(S["proj_loaded"], 16)
            for dst, src in ((cb_sb, cb), (qk1_sb, w_qk1), (v1w_sb, w_v1), (hsum_sb[:], head_sum), (out1_sb, w_out1)):
                sp.dma_start(dst, src).then_inc(S["middle_loaded"], 16)
            for dst, src in ((ff1_sb, w_ff1), (ff2_sb, w_ff2), (router_sb[:], w_router), (sg_sb, w_shared_gate),
                             (su_sb, w_shared_up), (sd_sb, w_shared_down), (before_sb[:], before)):
                sp.dma_start(dst, src).then_inc(S["last_loaded"], 16)
            sp.wait_ge(S["pads_ready"], 2)
            sp.dma_start(sorted_dram[E * SPAN * P:, :], pads[:]).then_inc(S["pad_tile_stored"], 16)

            def load_experts(first, last, done):
                for e in range(first, last):
                    sp.dma_start(we[:, e * EXPERT:(e + 1) * EXPERT], w_experts[e]).then_inc(S[done], 16)

            load_experts(0, RESIDENT, "experts_loaded")
            sp.wait_ge(S["ffn0_psum"], T)
            sp.wait_ge(S["out1_psum"], T)
            load_experts(RESIDENT, freed_by_b, "late_loaded")
            sp.wait_ge(S["ff2_psum"], 2 * T)
            load_experts(freed_by_b, freed_by_ff, "late_loaded")
            sp.wait_ge(S["down_psum"], T)
            load_experts(freed_by_ff, E, "late_loaded")

            def first_row(j):
                return sp.value_load(tile_row[0:1, bass.ds(j, 1)], min_val=0, max_val=E * SPAN * P)

            def load(s, first):
                sp.dma_start(xm[s], sorted_dram[bass.ds(first, P), 0:D]).then_inc(x_loaded[s], 16)

            def load_home(s, first):
                sp.dma_start(home[s][:], sorted_dram[bass.ds(first, P), D:ROW]).then_inc(home_loaded[s], 16)

            sp.wait_ge(S["table_ready"], 1)
            sp.sem_inc(S["unused"], 1)
            first = [first_row(s) for s in range(MOE_SLOTS)]
            sp.wait_ge(S["scattered"], 16 * T)
            sp.wait_ge(S["pad_tile_stored"], 16)
            sp.wait_ge(S["pads_stored"], 16 * E)
            for s in range(MOE_SLOTS):
                load(s, first[s])
            for s in range(MOE_SLOTS):
                load_home(s, first[s])

            def load_next(i):
                for s, j in tiles_of(i):
                    sp.wait_ge(S["xT_psum"], j - (MOE_SLOTS - 1))
                    sp.sem_inc(S["unused"], 1)
                    load(s, first_row(j))

            def load_next_home(i):
                for s, j in tiles_of(i):
                    sp.wait_ge(home_stored[s], i * 16)
                    sp.sem_inc(S["unused"], 1)
                    load_home(s, first_row(j))

            load_next(1)
            with sp.Fori(2, ROUNDS - 1) as i:
                load_next(i)
                load_next_home(i - 1)
            load_next(ROUNDS - 1)
            load_next_home(ROUNDS - 2)
            load_next_home(ROUNDS - 1)
            for s in range(MOE_SLOTS):
                rounds = ROUNDS if s < len(tiles_of(ROUNDS - 1)) else ROUNDS - 1
                sp.wait_ge(home_stored[s], 16 * rounds)

        @block.gpsimd
        def _(pool):
            pool.memset(pow_half[:], -0.5).then_inc(S["zero_ready"], 1)
            pool.memset(ln_eps[:], LN_EPS).then_inc(S["zero_ready"], 1)
            pool.memset(proj_sb[:], 0.0).then_inc(S["zero_ready"], 1)
            pool.memset(pads[:], 0.0).then_inc(S["pads_ready"], 1)
            pool.memset(ones_sb[:], 1.0).then_inc(S["consts_ready"], 1)
            pool.memset(ctxbd[:], 0.0).then_inc(S["consts_ready"], 1)
            pool.memset(voA[:], 1.0).then_inc(S["consts_ready"], 1)
            pool.memset(voB[:], 1.0).then_inc(S["consts_ready"], 1)
            pool.wait_ge(S["pads_ready"], 1)
            pool.memset(pads[:, 2 * D:ROW].bitcast(U32), NOWHERE).then_inc(S["pads_ready"], 1)

            def gather(t, done):
                pool.indirect_dma_start(out=H[:, t, :], out_offset=None, in_=table,
                                        in_offset=bass.IndirectOffsetOnAxis(ap=idx_sb[:, t:t + 1], axis=0)
                                        ).then_inc(done, 16)

            def gather_rest(t):
                if isinstance(t, int) and t == 0:
                    for later in range(GATHERED_ALONE, T):
                        gather(later, S["gathered_rest"])

            pool.wait_ge(S["idx_loaded"], 16)
            for t in range(GATHERED_ALONE):
                gather(t, gathered[t])
            pool.wait_ge(S["zero_ready"], 3)

            def inverse_deviation(k):
                def stage(t):
                    pool.wait_ge(var_ready[k], t + 1)
                    pool.tensor_tensor(rstd[:, k, 0:1], mv[:, k, 1:2], ln_eps[:], ALU.add).then_inc(pool_ln[k], 1)
                    pool.wait_ge(pool_ln[k], t + 1)
                    pool.tensor_tensor(rstd[:, k, 1:2], rstd[:, k, 0:1], pow_half[:],
                                       ALU.pow).then_inc(rstd_ready[k], 1)
                return stage

            def ahead_A(t):
                if isinstance(t, int):
                    pool.wait_ge(S["vectors_loaded"], 16)
                    pool.wait_ge(gathered[t] if t < GATHERED_ALONE else S["gathered_rest"],
                                 16 if t < GATHERED_ALONE else 16 * (T - GATHERED_ALONE))
                else:
                    pool.wait_ge(S["gathered_rest"], 16 * (T - GATHERED_ALONE))
                pool.tensor_tensor(preA[:], H[:, t, :], row["beta0"], ALU.add).then_inc(S["preA_ready"], 1)

            def ahead_A2(t):
                pool.tensor_tensor(preA[:], H[:, t, :], row["ffn0_bias"], ALU.add).then_inc(S["preA2_ready"], 1)

            def ahead_B(t):
                pool.wait_ge(src_ready[3], t + 1)
                pool.tensor_tensor(preB[:], yB[:], row["out1_bias"], ALU.add).then_inc(S["preB_ready"], 1)

            def reduce_kmax(t):
                pool.wait_ge(S["kmax_ready"], t + 1)
                pool.sem_inc(S["unused"], 1)
                pool.partition_all_reduce(kmax[:, 1, :], kmax[:, 0, :], P, MAX).then_inc(S["kmax_all"], 1)

            def ahead_C(t):
                pool.wait_ge(S["x1_ready"], t + 1)
                pool.tensor_tensor(preC[:], x1[:], row["b2"], ALU.add).then_inc(S["preC_ready"], 1)
                pool.tensor_tensor(H[:, t, :], H[:, t, :], row["be3"], ALU.add).then_inc(S["hC_ahead"], 1)

            def scatter(t):
                pool.wait_ge(S["slot_ready"], t * 2 + 2)
                pool.wait_ge(S["tile_done"], t + 1)
                pool.sem_inc(S["unused"], 1)
                pool.indirect_dma_start(out=sorted_dram, in_=send[:], in_offset=None,
                                        out_offset=bass.IndirectOffsetOnAxis(ap=slot_u[:], axis=0)
                                        ).then_inc(S["scattered"], 16)

            pool_ln = [sem(f"pool_ln{k}") for k in range(LN)]
            run_steps(pool, [
                (C, ahead_C), (B, inverse_deviation(3)), (A, inverse_deviation(0)), (A, ahead_A), (B, ahead_B),
                (B, reduce_kmax), (C, inverse_deviation(5)), (C, inverse_deviation(6)), (A, gather_rest),
                (A, inverse_deviation(1)), (A, inverse_deviation(2)), (A, ahead_A2), (B, inverse_deviation(4)),
                (C, scatter),
            ])

            pool.wait_ge(S["pads_known"], 1)
            for e in range(E):
                pool.indirect_dma_start(out=sorted_dram, in_=pads[:], in_offset=None,
                                        out_offset=bass.IndirectOffsetOnAxis(ap=pad_slots[:, e:e + 1], axis=0)
                                        ).then_inc(S["pads_stored"], 16)
            tokens_out = out.rearrange("t p d -> (t p) d")
            def store(i):
                for s, j in tiles_of(i):
                    pool.wait_ge(S["ey_ready"], j + 1)
                    pool.sem_inc(S["unused"], 1)
                    pool.indirect_dma_start(out=tokens_out, in_=ey[s], in_offset=None,
                                            out_offset=bass.IndirectOffsetOnAxis(
                                                ap=home[s][:, D:D + 1].bitcast(U32), axis=0),
                                            bounds_check=T * P - 1, oob_is_err=False).then_inc(home_stored[s], 16)

            with pool.Fori(0, ROUNDS - 1) as i:
                store(i)
            store(ROUNDS - 1)

        @block.scalar
        def _(act):
            def operand(k, dst, src):
                def stage(t):
                    act.wait_ge(srcT_psum[k], t + 1)
                    act.activation(flat(dst[:]), src[:, 0:D], ACT.Copy).then_inc(srcT_ready[k], 1)
                return stage

            def round_before(t):
                if isinstance(t, int) and t == 0:
                    act.wait_ge(S["last_loaded"], 16 * 7)
                    act.activation(before16[:], before_sb[:], ACT.Copy).then_inc(S["before_ready"], 1)

            def exp_min(t):
                act.wait_ge(S["xmin_ready"], t + 1)
                act.activation(qz[:].rearrange("p a b n -> p (a b n)"), qz[:].rearrange("p a b n -> p (a b n)"),
                               ACT.Exp).then_inc(S["exp_ready"], 1)

            def square(t):
                act.wait_ge(S["qk1_ready"], t + 1)
                act.activation(flat(sqB[:]), flat(qkB[:]), ACT.Square).then_inc(S["square_ready"], 1)

            def high_qk(t):
                act.wait_ge(S["qk1_ready"], t + 1)
                act.activation(flat(qkR[:, 0]), flat(qkB[:]), ACT.Copy).then_inc(S["qk_high"], 1)

            def high_proj(t):
                if isinstance(t, int) and t == 0:
                    act.wait_ge(S["proj_scaled"], 1)
                    act.activation(projR[:, 0], proj_sb[:], ACT.Copy).then_inc(S["proj_high"], 1)

            def read_xk(t):
                act.wait_ge(S["xk_psum"], t + 1)
                act.activation(flat(kf[:]), psB[:, 1:3, :].rearrange("p b n -> p (b n)"), ACT.Copy
                               ).then_inc(S["xk_read"], 1)

            def exp_q(t):
                act.wait_ge(S["qexp_in"], t + 1)
                act.activation(flat(qf[:]), flat(qf[:]), ACT.Exp).then_inc(S["qfeat_ready"], 1)

            def exp_k(t):
                act.wait_ge(S["kexp_in"], t + 1)
                act.activation(flat(kf[:]), flat(kf[:]), ACT.Exp).then_inc(S["kexp_out"], 1)

            def read_qT(t):
                act.wait_ge(S["qT_psum"], t + 1)
                act.activation(flat(qfT[:]), psB[:, 0:2, :].rearrange("p b n -> p (b n)"),
                               ACT.Copy, bias=EPS_K).then_inc(S["qT_ready"], 1)

            def relu(half):
                def stage(t):
                    act.wait_ge(S["ff1_psum"], t * 2 + (half + 1))
                    for f in range(4 * half, 4 * half + 4):
                        act.activation(ffT[:, f, :], psC[:, 1 - half, f % 4 * P:f % 4 * P + P], ACT.Relu,
                                       bias=b1_col[:, f:f + 1]).then_inc(S["ff_ready"], 1)
                return stage

            def tanh_top(t):
                act.wait_ge(S["logit_read"], t + 1)
                act.activation(top[:, 1:2], top[:, 0:1], ACT.Tanh, scale=0.5).then_inc(S["tanh_top"], 1)

            def tanh_gate(t):
                act.wait_ge(S["gate_psum"], t + 1)
                act.activation(tC[:], psC[:, 0, :], ACT.Tanh, scale=0.5).then_inc(S["tanh_gate"], 1)

            act.wait_ge(S["small_loaded"], 16 * 2)
            run_steps(act, [
                (C, operand(5, yTC, psC[:, 0, :])), (B, operand(3, yTB, psB[:, 0, :])),
                (A, operand(0, yTA, psA[:, 0, :])), (B, square), (B, high_qk), (C, relu(0)), (A, exp_min),
                (C, relu(1)), (B, read_xk), (B, exp_q), (B, exp_k), (A, operand(1, yTA, psA[:, 2, :])),
                (A, round_before), (B, read_qT), (C, operand(6, yTC, psC[:, 0, :])), (C, tanh_top), (C, tanh_gate),
                (B, operand(4, yTB, psB[:, 0, :])), (A, high_proj), (A, operand(2, yTA, psA[:, 0, :])),
            ])

            def read_xT(i):
                for s, j in tiles_of(i):
                    act.wait_ge(S["xT_psum"], j + 1)
                    act.activation(flat(xT[s]), banks_of[s][0][:, 0:D], ACT.Copy).then_inc(S["xT_ready"], 1)

            def expert_tiles(i, following):
                for s, j in tiles_of(i):
                    act.wait_ge(S["eg_psum"], j + 1)
                    act.activation(eg1[s], banks_of[s][1], ACT.Tanh, scale=0.5).then_inc(S["tanh_eg"], 1)
                for k in following:
                    read_xT(k)
                for s, j in tiles_of(i):
                    act.wait_ge(S["ehT_psum"], j + 1)
                    act.activation(flat(ehT[s]), banks_of[s][3], ACT.Copy).then_inc(S["ehT_ready"], 1)

            read_xT(0)
            with act.Fori(0, ROUNDS - 2) as i:
                expert_tiles(i, [i + 1])
            expert_tiles(ROUNDS - 2, [ROUNDS - 1])
            expert_tiles(ROUNDS - 1, [])

        @block.vector
        def _(dve):
            links = [0, 0, 0]

            def link(p, t, ins):
                links[p] += 1
                ins.then_inc(dve_step[p], 1)
                dve.wait_ge(dve_step[p], t * LINKS[p] + links[p])

            def begins(p):
                assert links[p] in (0, LINKS[p]), (p, links)
                links[p] = 0

            def norm_stats(k, p, src, t):
                dve.sem_inc(S["unused"], 1)
                link(p, t, dve.bn_stats(stats[:, k], src))
                dve.sem_inc(S["unused"], 1)
                dve.bn_aggr(mv[:, k], stats[:, k]).then_inc(var_ready[k], 1)

            def normalise(dst, src, k, t):
                dve.wait_ge(rstd_ready[k], t + 1)
                return dve.tensor_scalar(dst, src, mv[:, k, 0:1], rstd[:, k, 1:2], ALU.subtract, ALU.mult)

            def weighted_mean(p, t, bank, den, eps, dst, k):
                h = heads(bank)
                link(p, t, dve.tensor_scalar(den[:, 0, :], h[:, :, DH], eps, None, ALU.add))
                link(p, t, dve.reciprocal(den[:, 1, :], den[:, 0, :]))
                dve.tensor_tensor(dst[:].rearrange("p (h c) -> p h c", h=HEADS), h[:, :, 0:DH],
                                  by_head(den[:, 1, :], DH), ALU.mult).then_inc(src_ready[k], 1)

            def values(dst, bank, bias, done):
                dve.tensor_tensor(dst[:, :, 0:DH], bank[:, 0:D].rearrange("p (h c) -> p h c", h=HEADS),
                                  bias.rearrange("p (h c) -> p h c", h=HEADS), ALU.add).then_inc(S[done], 1)

            def a_stats(t):
                begins(0)
                if isinstance(t, int) and t < GATHERED_ALONE:
                    dve.wait_ge(gathered[t], 16)
                else:
                    dve.wait_ge(S["gathered_rest"], 16 * (T - GATHERED_ALONE))
                norm_stats(0, 0, H[:, t, :], t)

            def a_norm(t):
                normalise(yA[:], H[:, t, :], 0, t).then_inc(src_ready[0], 1)

            def a_qkv(t):
                dve.wait_ge(S["qk0_psum"], t + 1)
                link(0, t, dve.tensor_tensor(xA[:], by4(psA[:, 1, :]), chunk_bias(qk0_bias, 4), ALU.add))
                dve.tensor_scalar(qz[:].rearrange("p a b n -> p (a b) n"), xA[:], 0.0, None,
                                  ALU.min).then_inc(S["xmin_ready"], 1)
                dve.wait_ge(S["v0_psum"], t + 1)
                values(voA, psA[:, 2, :], row["v0_bias"], "v0_ready")

            def a_elu(t):
                dve.wait_ge(S["exp_ready"], t + 1)
                link(0, t, dve.scalar_tensor_tensor(out=qkA[:], in0=xA[:], scalar=0.0,
                                                    in1=qz[:].rearrange("p a b n -> p (a b) n"),
                                                    op0=ALU.max, op1=ALU.add))
                for a in range(2):
                    link(0, t, dve.tensor_scalar(qz[:, :, a, :], qkA[:, 0:KD, :], FEAT_EPS, parity[:, a:a + 1],
                                                 ALU.add, ALU.mult))
                dve.tensor_scalar(qkA[:, KD:4, :], qkA[:, KD:4, :], FEAT_EPS, None,
                                  ALU.add).then_inc(S["qk0_ready"], 1)

            def a_mask(t):
                for b in range(4):
                    dve.wait_ge(S["scores_psum"], t * 4 + (b + 1))
                    dve.tensor_tensor(S_sb[:, b], by4(psA[:, b % 3, :]),
                                      causal_sb[:].unsqueeze(1).broadcast_to([P, 4, P]), ALU.mult
                                      ).then_inc(S["scores_masked"], 1)

            def a_mean(t):
                dve.wait_ge(S["heads0_psum"], t * 4 + 4)
                weighted_mean(0, t, psA[:, 1, :], denA, 4 * FEAT_EPS, tmpA, 1)

            def a_out(t):
                dve.wait_ge(S["out0_psum"], t + 1)
                link(0, t, dve.tensor_tensor(tmpA[:], psA[:, 0, 0:D], row["out0_bias"], ALU.add))
                norm_stats(1, 0, tmpA[:], t)

            def a_residual(t):
                link(0, t, normalise(tmpA[:], tmpA[:], 1, t))
                link(0, t, dve.tensor_tensor(tmpA[:], tmpA[:], row["gamma0"], ALU.mult))
                dve.wait_ge(S["preA_ready"], t + 1)
                link(0, t, dve.tensor_tensor(H[:, t, :], tmpA[:], preA[:], ALU.add))
                norm_stats(2, 0, H[:, t, :], t)

            def a_norm2(t):
                normalise(yA[:], H[:, t, :], 2, t).then_inc(src_ready[2], 1)

            def a_ffn(t):
                dve.wait_ge(S["ffn0_psum"], t + 1)
                link(0, t, dve.tensor_tensor(tmpA[:], psA[:, 1, 0:D], row["ffn0_scb"], ALU.mult))
                dve.wait_ge(S["preA2_ready"], t + 1)
                link(0, t, dve.tensor_tensor(H[:, t, :], tmpA[:], preA[:], ALU.add))

            def b_stats(t):
                begins(1)
                norm_stats(3, 1, H[:, t, :], t)

            def b_norm(t):
                normalise(yB[:], H[:, t, :], 3, t).then_inc(src_ready[3], 1)

            def b_qkv(t):
                dve.wait_ge(S["qk1_psum"], t + 1)
                dve.tensor_tensor(qkB[:], by4(psB[:, 1, :]), chunk_bias(qk1_bias, 4), ALU.add
                                  ).then_inc(S["qk1_ready"], 1)
                dve.wait_ge(S["v1_psum"], t + 1)
                values(voB, psB[:, 2, :], row["v1_bias"], "v1_ready")

            def b_low_qk(t):
                dve.wait_ge(S["qk_high"], t + 1)
                dve.tensor_tensor(flat(qkR[:, 1]), flat(qkB[:]), flat(qkR[:, 0]).bitcast(F32), ALU.subtract
                                  ).then_inc(S["qk_split"], 1)

            def b_kmax(t):
                dve.wait_ge(S["diag_psum"], t + 1)
                dve.tensor_copy(flat(diag[:]), psB[:, 0, 0:2 * HEADS]).then_inc(S["diag_read"], 1)
                dve.wait_ge(S["xk_read"], t + 1)
                dve.tensor_reduce(kmax[:, 0, :], kf[:], AX.X, ALU.max).then_inc(S["kmax_ready"], 1)

            def b_q(t):
                xq = psB[:, 0:2, :].rearrange("p b (h m) -> p (b h) m", m=M)
                dve.wait_ge(S["xq_psum"], t + 1)
                link(1, t, dve.tensor_reduce(qmax[:, 0, :], xq, AX.X, ALU.max))
                link(1, t, dve.tensor_tensor(qmax[:, 1, :], qmax[:, 0, :], diag[:, 0, :], ALU.add))
                dve.tensor_tensor(qf[:], xq, by_head(qmax[:, 1, :], M), ALU.subtract).then_inc(S["qexp_in"], 1)

            def b_k(t):
                dve.wait_ge(S["kmax_all"], t + 1)
                link(1, t, dve.tensor_tensor(kmax[:, 2, :], kmax[:, 1, :], diag[:, 1, :], ALU.add))
                dve.tensor_tensor(kf[:], kf[:], by_head(kmax[:, 2, :], M), ALU.subtract).then_inc(S["kexp_in"], 1)

            def b_keps(t):
                dve.wait_ge(S["kexp_out"], t + 1)
                dve.tensor_scalar(kf[:], kf[:], EPS_K, None, ALU.add).then_inc(S["kfeat_ready"], 1)

            def b_ctx(t):
                dve.wait_ge(S["ctx_psum"], t * 4 + 4)
                pairs = psB[:, 2, 0:PAIRS * 2 * V1].rearrange("p (a v) -> p a v", a=PAIRS)
                for a in range(2):
                    dve.tensor_copy(ctxbd[M * a:M * a + M, :, V1 * a:V1 * a + V1],
                                    pairs[M * a:M * a + M, :, V1 * a:V1 * a + V1]).then_inc(S["ctx_ready"], 1)

            def b_mean(t):
                dve.wait_ge(S["heads1_psum"], t * 4 + 4)
                weighted_mean(1, t, psB[:, 2, :], denB, 0.0, tmpB, 4)

            def b_out(t):
                dve.wait_ge(S["out1_psum"], t + 1)
                dve.wait_ge(S["preB_ready"], t + 1)
                link(1, t, dve.tensor_tensor(tmpB[:], psB[:, 1, 0:D], preB[:], ALU.add))
                norm_stats(4, 1, tmpB[:], t)

            def b_x(t):
                link(1, t, normalise(tmpB[:], tmpB[:], 4, t))
                link(1, t, dve.tensor_tensor(tmpB[:], tmpB[:], row["g2"], ALU.mult))
                dve.tensor_tensor(x1[:], tmpB[:], row["be2"], ALU.add).then_inc(S["x1_ready"], 1)

            def c_ff(t):
                begins(2)
                dve.wait_ge(S["ff2_psum"], t * 2 + 2)
                dve.wait_ge(S["preC_ready"], t + 1)
                link(2, t, dve.tensor_tensor(tmpC[:], psC[:, 1, 0:D], preC[:], ALU.add))
                norm_stats(5, 2, tmpC[:], t)

            def c_residual(t):
                link(2, t, normalise(tmpC[:], tmpC[:], 5, t))
                link(2, t, dve.tensor_tensor(tmpC[:], tmpC[:], row["g3"], ALU.mult))
                dve.wait_ge(S["hC_ahead"], t + 1)
                link(2, t, dve.tensor_tensor(H[:, t, :], tmpC[:], H[:, t, :], ALU.add))
                norm_stats(6, 2, H[:, t, :], t)

            def c_norm(t):
                normalise(yC[:], H[:, t, :], 6, t).then_inc(src_ready[6], 1)

            def c_logits(t):
                dve.wait_ge(S["logit_psum"], t + 1)
                link(2, t, dve.tensor_copy(lg[:], psC[:, 1, 0:E]))
                link(2, t, dve.tensor_reduce(top[:, 0:1], lg[:], AX.X, ALU.max))
                dve.sem_inc(S["logit_read"], 1)

            def c_choose(t):
                link(2, t, dve.tensor_scalar(mark[:], lg[:], top[:, 0:1], None, ALU.is_equal))
                link(2, t, dve.tensor_tensor(mark[:], mark[:], rev, ALU.mult))
                link(2, t, dve.tensor_reduce(top[:, 3:4], mark[:], AX.X, ALU.max))
                dve.tensor_scalar(onehot[:], rev, top[:, 3:4], None, ALU.is_equal).then_inc(S["onehot_ready"], 1)

            def c_slot(t):
                dve.wait_ge(S["count_psum"], t + 1)
                link(2, t, dve.tensor_tensor(rank[:, 0, :], psC[:, 1, 0:E], base[:], ALU.add))
                link(2, t, dve.tensor_tensor(base[:], psC[:, 1, E:2 * E], base[:], ALU.add))
                link(2, t, dve.tensor_tensor(rank[:, 1, :], rank[:, 0, :], onehot[:], ALU.mult))
                link(2, t, dve.tensor_reduce(slot[:], rank[:, 1, :], AX.X, ALU.add))
                dve.tensor_copy(send[:, 2 * D:ROW].bitcast(U32), token[:]).then_inc(S["slot_ready"], 1)
                dve.wait_ge(S["slot_ready"], t * 2 + 1)
                link(2, t, dve.tensor_scalar(token[:], token[:], float(P), None, ALU.add))
                dve.tensor_copy(slot_u[:], slot[:]).then_inc(S["slot_ready"], 1)

            def c_hidden(t):
                dve.wait_ge(S["tanh_top"], t + 1)
                link(2, t, dve.tensor_scalar(top[:, 2:3], top[:, 1:2], 0.5, 0.5, ALU.mult, ALU.add))
                dve.wait_ge(S["scattered"], t * 16)
                link(2, t, dve.tensor_scalar(send[:, 0:D], yC[:], top[:, 2:3], None, ALU.mult))
                dve.wait_ge(S["tanh_gate"], t + 1)
                link(2, t, dve.scalar_tensor_tensor(out=gC[:], in0=tC[:], scalar=1.0, in1=psC[:, 0, :],
                                                    op0=ALU.add, op1=ALU.mult))
                dve.wait_ge(S["up_psum"], t + 1)
                dve.scalar_tensor_tensor(out=flat(hT[:]), in0=gC[:], scalar=0.5, in1=psC[:, 1, :],
                                         op0=ALU.mult, op1=ALU.mult).then_inc(S["hT_ready"], 1)

            def c_down(t):
                dve.wait_ge(S["down_psum"], t + 1)
                link(2, t, dve.tensor_tensor(send[:, D:2 * D], psC[:, 0, 0:D], H[:, t, :], ALU.add))
                dve.sem_inc(S["tile_done"], 1)

            def prepare(t):
                if isinstance(t, int) and t == 0:
                    dve.tensor_copy(base[:], start_row).then_inc(S["prepared"], 1)
                    dve.tensor_copy(token[:], partition).then_inc(S["prepared"], 1)
                    dve.wait_ge(S["consts_ready"], 4)
                    dve.wait_ge(S["vectors_loaded"], 16)
                    dve.tensor_scalar(row["ffn0_scb"], row["ffn0_scb"], 1.0 / 127.0, None,
                                      ALU.mult).then_inc(S["prepared"], 1)
                    dve.wait_ge(S["prepared"], 3)

            def prepare_proj(t):
                if isinstance(t, int) and t == 0:
                    dve.wait_ge(S["proj_loaded"], 16 * 8)
                    dve.tensor_scalar(proj_sb[:], proj_sb[:], float(DH) ** -0.25, None,
                                      ALU.mult).then_inc(S["proj_scaled"], 1)

            def low_proj(t):
                if isinstance(t, int) and t == 0:
                    dve.wait_ge(S["proj_high"], 1)
                    dve.tensor_tensor(projR[:, 1], proj_sb[:], projR[:, 0].bitcast(F32), ALU.subtract
                                      ).then_inc(S["proj_split"], 1)

            dve.wait_ge(S["small_loaded"], 16 * 2)
            run_steps(dve, [
                (B, b_stats), (A, a_stats), (B, b_norm), (A, a_norm), (A, prepare), (B, b_qkv), (A, a_qkv),
                (B, b_low_qk), (A, a_elu), (B, b_kmax), (A, prepare_proj), (A, a_mask), (B, b_q), (B, b_k), (C, c_ff),
                (B, b_keps), (A, a_mean), (C, c_residual), (B, b_ctx), (C, c_norm), (A, a_out), (B, b_mean),
                (A, a_residual), (C, c_logits), (C, c_choose), (A, a_norm2), (C, c_hidden), (B, b_out), (C, c_slot),
                (B, b_x), (A, a_ffn), (A, low_proj), (C, c_down),
            ])
            steps = [0]

            def then(ins):
                steps[0] += 1
                ins.then_inc(S["table_step"], 1)
                dve.wait_ge(S["table_step"], steps[0])

            first_tile, need, behind = rt[:, 0:E], rt[:, E:2 * E], [rt[:, 2 * E:3 * E], rt[:, 3 * E:4 * E]]
            count, shift = rt[:, 4 * E:5 * E], rt[:, 5 * E:6 * E]
            exceeds = flatS[:, 0:E * T].rearrange("p (e k) -> p e k", e=E)
            ended, begun, where = (flatS[:, 1024 * n:1024 * n + SORTED_TILES * E].rearrange("p (j e) -> p j e", e=E)
                                   for n in (0, 1, 1))
            sums = flatS[:, 512:512 + 3 * SORTED_TILES].rearrange("p (n j) -> p n j", n=3)

            def by_tile(v):
                return v.unsqueeze(1).broadcast_to([P, SORTED_TILES, E])

            tiles = number.unsqueeze(2).broadcast_to([P, SORTED_TILES, E])
            then(dve.tensor_tensor(pad_slots[:], base[:], partition.broadcast_to([P, E]), ALU.add))
            dve.sem_inc(S["pads_known"], 1)
            then(dve.tensor_tensor(count, base[:], start_row, ALU.subtract))
            then(dve.tensor_tensor(exceeds, count.unsqueeze(2).broadcast_to([P, E, T]),
                                   full.unsqueeze(1).broadcast_to([P, E, T]), ALU.is_gt))
            then(dve.tensor_reduce(need, exceeds, AX.X, ALU.add))
            src, d = need, 1
            while d < E:
                dst = behind[0] if src is not behind[0] else behind[1]
                then(dve.tensor_copy(dst[:, 0:d], src[:, 0:d]))
                then(dve.tensor_tensor(dst[:, d:E], src[:, d:E], src[:, 0:E - d], ALU.add))
                src, d = dst, 2 * d
            ends = src
            then(dve.tensor_tensor(first_tile, ends, need, ALU.subtract))
            then(dve.tensor_tensor(ended, by_tile(ends), tiles, ALU.is_le))
            then(dve.tensor_reduce(sums[:, 0, :], ended, AX.X, ALU.add))
            then(dve.tensor_scalar(tile_expert, sums[:, 0, :], float(E - 1), None, ALU.min))
            then(dve.tensor_tensor(begun, by_tile(first_tile), tiles, ALU.is_le))
            then(dve.tensor_tensor(begun, begun, ended, ALU.subtract))
            then(dve.tensor_scalar(shift, first_tile, float(-P), float(-E * SPAN * P), ALU.mult, ALU.add))
            then(dve.tensor_tensor(shift, shift, start_row, ALU.add))
            then(dve.tensor_tensor(ended, begun, by_tile(shift), ALU.mult))
            then(dve.tensor_reduce(sums[:, 0, :], ended, AX.X, ALU.add))
            then(dve.tensor_tensor(ended, begun, tiles, ALU.mult))
            then(dve.tensor_reduce(sums[:, 1, :], ended, AX.X, ALU.add))
            then(dve.tensor_scalar(sums[:, 1, :], sums[:, 1, :], float(P), float(E * SPAN * P), ALU.mult, ALU.add))
            then(dve.tensor_tensor(tile_row, sums[:, 0, :], sums[:, 1, :], ALU.add))
            dve.sem_inc(S["table_ready"], 1)

            def expert_tiles(i):
                for s, j in tiles_of(i):
                    dve.wait_ge(S["tanh_eg"], j + 1)
                    dve.scalar_tensor_tensor(out=eg2[s], in0=eg1[s], scalar=1.0, in1=banks_of[s][1],
                                             op0=ALU.add, op1=ALU.mult).then_inc(S["eg_ready"], 1)
                    dve.wait_ge(S["eg_ready"], j + 1)
                    dve.wait_ge(S["eu_psum"], j + 1)
                    dve.scalar_tensor_tensor(out=flat(eh[s]), in0=eg2[s], scalar=0.5, in1=banks_of[s][2],
                                             op0=ALU.mult, op1=ALU.mult).then_inc(S["eh_ready"], 1)
                for s, j in tiles_of(i):
                    dve.wait_ge(S["ey_psum"], j + 1)
                    dve.wait_ge(home_loaded[s], i * 16 + 16)
                    dve.tensor_tensor(ey[s], banks_of[s][3][:, 0:D], home[s][:, 0:D], ALU.add
                                      ).then_inc(S["ey_ready"], 1)

            with dve.Fori(0, ROUNDS - 1) as i:
                expert_tiles(i)
            expert_tiles(ROUNDS - 1)

        @block.tensor
        def _(pe):
            def matmul(o, a, b, start, stop):
                return pe.matmul(o, a, b, start=start, stop=stop)

            def transposed(k, dst, src):
                def stage(t):
                    pe.wait_ge(S["x1_ready"] if k == 5 else src_ready[k], t + 1)
                    if k == 5:
                        pe.wait_ge(S["tile_done"], t)
                    for c in range(KD):
                        ins = pe.transpose(dst[:, c * P:(c + 1) * P], src[:, c * P:(c + 1) * P], id_sb[:])
                    ins.then_inc(srcT_psum[k], 1)
                return stage

            def by_token(o, a, b, chunks):
                for c in range(chunks):
                    ins = matmul(o, a[:, c, :], b[:, c, :], c == 0, c == chunks - 1)
                return ins

            def by_channel(bank, yT, w, blocks):
                for n, m in enumerate(blocks):
                    for c in range(KD):
                        ins = matmul(bank[:, n * P:(n + 1) * P], w[:, c, m * P:(m + 1) * P], yT[:, c, :],
                                     c == 0, c == KD - 1)
                return ins

            def a_qkv(t):
                pe.wait_ge(srcT_ready[0], t + 1)
                by_channel(psA[:, 1, :], yTA, qk0_sb, range(4)).then_inc(S["qk0_psum"], 1)
                by_token(psA[:, 2, 0:D], yTA, v0_sb, KD).then_inc(S["v0_psum"], 1)

            def a_scores(b):
                def stage(t):
                    if b == 0:
                        pe.wait_ge(S["qk0_ready"], t + 1)
                        pe.wait_ge(S["v0_ready"], t + 1)
                    if b == 3:
                        pe.wait_ge(S["scores_masked"], t * 4 + 1)
                    rows_of = slice(32 * b, 32 * b + 32)
                    for half in range(2):
                        ins = matmul(psA[:, b % 3, half * 256:half * 256 + 256], qkA[rows_of, KD + half, :],
                                     qz[rows_of, half].rearrange("p a n -> p (a n)"), True, True)
                    ins.then_inc(S["scores_psum"], 1)
                return stage

            def a_heads(b):
                def stage(t):
                    pe.wait_ge(S["scores_masked"], t * 4 + max(b + 1, 2))
                    for half in range(2):
                        for a in range(2):
                            h = 2 * (4 * half + b) + a
                            ins = matmul(heads(psA[:, 1, :])[:, h, :], S_sb[:, b, 2 * half + a, :], voA[:, h, :],
                                         True, True)
                    ins.then_inc(S["heads0_psum"], 1)
                return stage

            def a_out(t):
                pe.wait_ge(srcT_ready[1], t + 1)
                by_token(psA[:, 0, 0:D], yTA, out0_sb, KD).then_inc(S["out0_psum"], 1)

            def a_ffn(t):
                pe.wait_ge(srcT_ready[2], t + 1)
                by_token(psA[:, 1, 0:D], yTA, cb_sb, KD).then_inc(S["ffn0_psum"], 1)

            def b_qkv(t):
                pe.wait_ge(srcT_ready[3], t + 1)
                by_channel(psB[:, 1, :], yTB, qk1_sb, range(4)).then_inc(S["qk1_psum"], 1)
                by_token(psB[:, 2, 0:D], yTB, v1w_sb, KD).then_inc(S["v1_psum"], 1)

            def features(bank, chunk):
                for n, (x, w) in enumerate(((0, 0), (0, 1), (1, 0))):
                    ins = matmul(bank, qkR[:, x, chunk, :], projR[:, w], n == 0, n == 2)
                return ins

            def b_diag(t):
                pe.wait_ge(S["square_ready"], t + 1)
                for c in range(4):
                    ins = matmul(psB[:, 0, 8 * c:8 * c + 8], sqB[:, c, :], hsum_sb[:], True, True)
                ins.then_inc(S["diag_psum"], 1)

            def b_k(t):
                pe.wait_ge(S["v1_ready"], t + 1)
                pe.wait_ge(S["qk_split"], t + 1)
                for c in range(KD):
                    ins = features(psB[:, 1 + c, :], KD + c)
                ins.then_inc(S["xk_psum"], 1)

            def b_q(t):
                pe.wait_ge(S["diag_read"], t + 1)
                pe.wait_ge(S["xk_read"], t + 1)
                for c in range(KD):
                    ins = features(psB[:, c, :], c)
                ins.then_inc(S["xq_psum"], 1)

            def b_qT(t):
                pe.wait_ge(S["qfeat_ready"], t + 1)
                for pair in range(PAIRS):
                    ins = pe.transpose(psB[:, pair // 4, pair % 4 * P:pair % 4 * P + P],
                                       flat(qf[:])[:, pair * P:(pair + 1) * P], id_sb[:])
                ins.then_inc(S["qT_psum"], 1)

            def b_ctx(quarter):
                def stage(t):
                    if quarter == 0:
                        pe.wait_ge(S["kfeat_ready"], t + 1)
                    for pair in range(2 * quarter, 2 * quarter + 2):
                        ins = matmul(psB[:, 2, pair * 2 * V1:(pair + 1) * 2 * V1],
                                     flat(kf[:])[:, pair * P:(pair + 1) * P],
                                     flat(voB[:, 2 * pair:2 * pair + 2, :]), True, True)
                    ins.then_inc(S["ctx_psum"], 1)
                return stage

            def b_heads(quarter):
                def stage(t):
                    if quarter == 0:
                        pe.wait_ge(S["ctx_ready"], t * 2 + 2)
                        pe.wait_ge(S["qT_ready"], t + 1)
                    for pair in range(2 * quarter, 2 * quarter + 2):
                        ins = matmul(psB[:, 2, pair * 2 * V1:(pair + 1) * 2 * V1], qfT[:, pair, :],
                                     ctxbd[:, pair, :], True, True)
                    ins.then_inc(S["heads1_psum"], 1)
                return stage

            def b_out(t):
                pe.wait_ge(srcT_ready[4], t + 1)
                by_token(psB[:, 1, 0:D], yTB, out1_sb, KD).then_inc(S["out1_psum"], 1)

            def c_ff1(half):
                def stage(t):
                    pe.wait_ge(srcT_ready[5], t + 1)
                    by_channel(psC[:, 1 - half, :], yTC, ff1_sb, range(4 * half, 4 * half + 4)
                               ).then_inc(S["ff1_psum"], 1)
                return stage

            def c_ff2(half):
                def stage(t):
                    pe.wait_ge(S["ff_ready"], t * KF + KF)
                    for c in range(KF // 2 * half, KF // 2 * (half + 1)):
                        ins = matmul(psC[:, 1, 0:D], ffT[:, c, :], ff2_sb[:, c, :], c == 0, c == KF - 1)
                    ins.then_inc(S["ff2_psum"], 1)
                return stage

            def c_gate(t):
                pe.wait_ge(srcT_ready[6], t + 1)
                by_token(psC[:, 1, 0:E], yTC, router_sb, KD).then_inc(S["logit_psum"], 1)
                by_channel(psC[:, 0, :], yTC, sg_sb, range(KE)).then_inc(S["gate_psum"], 1)

            def c_up(t):
                pe.wait_ge(S["logit_read"], t + 1)
                by_channel(psC[:, 1, :], yTC, su_sb, range(KE)).then_inc(S["up_psum"], 1)

            def c_count(t):
                pe.wait_ge(S["hT_ready"], t + 1)
                pe.wait_ge(S["onehot_ready"], t + 1)
                matmul(psC[:, 1, 0:E], before16[:], onehot[:], True, True)
                matmul(psC[:, 1, E:2 * E], ones_sb[:], onehot[:], True, True).then_inc(S["count_psum"], 1)

            def c_down(t):
                pe.wait_ge(S["hT_ready"], t + 1)
                by_token(psC[:, 0, 0:D], hT, sd_sb, KE).then_inc(S["down_psum"], 1)

            def once(stage, name, value):
                def first(t):
                    if not isinstance(t, int) or t == 0:
                        pe.wait_ge(S[name], value)
                    stage(t)
                return first

            pe.wait_ge(S["small_loaded"], 16 * 2)
            run_steps(pe, [
                (C, transposed(5, psC[:, 0, :], x1)), (C, once(c_ff1(0), "last_loaded", 16 * 7)),
                (B, transposed(3, psB[:, 0, :], yB)), (A, transposed(0, psA[:, 0, :], yA)),
                (B, once(b_qkv, "middle_loaded", 16 * 5)), (A, once(a_qkv, "qkv0_loaded", 16 * 2)), (B, b_diag),
                (C, c_ff1(1)), (B, once(b_k, "proj_split", 1)), (A, once(a_scores(0), "out0_loaded", 16 * 2)),
                (A, a_scores(1)), (B, b_q), (A, a_scores(2)), (A, a_scores(3)), (A, a_heads(0)), (C, c_ff2(0)),
                (A, a_heads(1)), (C, c_ff2(1)), (A, a_heads(2)), (A, a_heads(3)), (B, b_qT), (B, b_ctx(0)),
                (A, transposed(1, psA[:, 2, :], tmpA)), (B, b_ctx(1)), (B, b_ctx(2)), (B, b_ctx(3)), (A, a_out),
                (B, b_heads(0)), (B, b_heads(1)), (C, transposed(6, psC[:, 0, :], yC)), (B, b_heads(2)),
                (B, b_heads(3)), (C, c_gate), (B, transposed(4, psB[:, 0, :], tmpB)), (C, c_up), (B, b_out),
                (A, transposed(2, psA[:, 0, :], yA)), (C, once(c_count, "before_ready", 1)),
                (A, once(a_ffn, "middle_loaded", 16 * 5)), (C, c_down),
            ])
            pe.wait_ge(S["table_ready"], 1)
            pe.wait_ge(S["experts_loaded"], 16 * RESIDENT)
            pe.wait_ge(S["late_loaded"], 16 * (E - RESIDENT))

            def transpose_x(i):
                for s, _ in tiles_of(i):
                    pe.wait_ge(x_loaded[s], i * 16 + 16)
                    for c in range(KD):
                        ins = pe.transpose(banks_of[s][0][:, c * P:(c + 1) * P], xm[s][:, c * P:(c + 1) * P], id_sb[:])
                    ins.then_inc(S["xT_psum"], 1)

            def expert_tiles(i, following):
                expert = [pe.value_load(tile_expert[0:1, bass.ds(j, 1)], min_val=0, max_val=E - 1)
                          for _, j in tiles_of(i)]
                for s, j in tiles_of(i):
                    pe.wait_ge(S["xT_ready"], j + 1)
                    for b, at, done in ((1, GATE, "eg_psum"), (2, UP, "eu_psum")):
                        for c in range(KD):
                            ins = matmul(banks_of[s][b], xT[s][:, c, :],
                                         we[:, bass.ds(expert[s] * EXPERT + (at + c * F), F)], c == 0, c == KD - 1)
                        ins.then_inc(S[done], 1)
                for k in following:
                    transpose_x(k)
                for s, j in tiles_of(i):
                    pe.wait_ge(S["eh_ready"], j + 1)
                    for c in range(KE):
                        ins = pe.transpose(banks_of[s][3][:, c * P:(c + 1) * P], eh[s][:, c, :], id_sb[:])
                    ins.then_inc(S["ehT_psum"], 1)
                for s, j in tiles_of(i):
                    pe.wait_ge(S["ehT_ready"], j + 1)
                    for c in range(KE):
                        ins = matmul(banks_of[s][3][:, 0:D], ehT[s][:, c, :],
                                     we[:, bass.ds(expert[s] * EXPERT + (DOWN + c * D), D)], c == 0, c == KE - 1)
                    ins.then_inc(S["ey_psum"], 1)

            transpose_x(0)
            with pe.Fori(0, ROUNDS - 2) as i:
                expert_tiles(i, [i + 1])
            expert_tiles(ROUNDS - 2, [ROUNDS - 1])
            expert_tiles(ROUNDS - 1, [])

    return nc


def kernel(**inputs):
    import numpy as np
    import concourse.bacc as bacc
    from concourse.bass_utils import run_bass_kernel_spmd

    a = {k: np.asarray(v) for k, v in inputs.items()}

    def chunks(w):
        return np.ascontiguousarray(w.reshape(-1, 128, w.shape[1]).transpose(1, 0, 2))

    def column(v):
        return v.reshape(-1, 128).T

    D = a["L0_tok_weight"].shape[1]
    E = a["L1_ffn_router_w"].shape[0]
    T = a["x"].shape[0]
    qkv0, b0 = a["L0_attn_Wqkv"], a["L0_attn_bqkv"]
    f4 = np.float32
    part = np.arange(128)
    parity = np.stack([part // 16 % 2 == 0, part // 16 % 2 == 1], 1).astype(f4)
    counts = np.concatenate([E - np.arange(E), 128 * np.arange(T), np.arange(T + E - 1),
                             128 * (T + 1) * np.arange(E)]).astype(f4)
    experts = np.concatenate([
        a["L1_ffn_expert_gate"].reshape(E, D // 128, 128, -1).transpose(0, 2, 1, 3).reshape(E, 128, -1),
        a["L1_ffn_expert_up"].reshape(E, D // 128, 128, -1).transpose(0, 2, 1, 3).reshape(E, 128, -1),
        a["L1_ffn_expert_down"].reshape(E, -1, 128, D).transpose(0, 2, 1, 3).reshape(E, 128, -1)], axis=2)
    arrays = {
        "idx": np.ascontiguousarray(a["x"].T.view(np.uint32)),
        "table": a["L0_tok_weight"],
        "w_qk0": chunks(qkv0[0:2 * D].T), "w_v0": chunks(qkv0[2 * D:].T), "w_out0": chunks(a["L0_attn_Wout"].T),
        "cb": chunks(a["L0_ffn_CB"].T),
        "w_qk1": chunks(np.concatenate([a["L1_attn_Wq"], a["L1_attn_Wk"]]).T),
        "w_v1": chunks(a["L1_attn_Wv"].T), "w_out1": chunks(a["L1_attn_Wo"].T),
        "proj": np.ascontiguousarray(a["L1_attn_proj"].T),
        "w_ff1": chunks(a["L1_attn_W1"].T), "w_ff2": chunks(a["L1_attn_W2"].T),
        "w_router": chunks(a["L1_ffn_router_w"].T),
        "w_shared_gate": chunks(a["L1_ffn_shared_gate"]), "w_shared_up": chunks(a["L1_ffn_shared_up"]),
        "w_shared_down": chunks(a["L1_ffn_shared_down"]),
        "w_experts": experts,
        "rows": np.stack([b0[2 * D:], a["L0_attn_bout"], a["L0_attn_gamma"], a["L0_attn_beta"], a["L0_ffn_SCB"],
                          a["L0_ffn_bias"], a["L1_attn_bv"], a["L1_attn_bo"], a["L1_attn_g2"], a["L1_attn_be2"],
                          a["L1_attn_b2"], a["L1_attn_g3"], a["L1_attn_be3"]]),
        "cols": np.concatenate([column(b0[0:2 * D]), column(a["L1_attn_bq"]), column(a["L1_attn_bk"]),
                                column(a["L1_attn_b1"]), parity, np.broadcast_to(counts, (128, counts.size)),
                                part[:, None].astype(f4)], axis=1),
        "ident": np.eye(128, dtype=f4),
        "causal": (part[:, None] <= part[None, :]).astype(f4),
        "head_sum": 0.125 * (part[:, None] // 16 == np.arange(8)[None, :]).astype(f4),
        "before": (part[:, None] < part[None, :]).astype(f4),
    }
    nc = bacc.Bacc("TRN2", target_bir_lowering=False, num_devices=1)
    arrays = {k: np.ascontiguousarray(v) for k, v in arrays.items()}
    args = [nc.dram_tensor(k, v.shape, mybir.dt.from_np(v.dtype), kind="ExternalInput").ap() for k, v in arrays.items()]
    out = nc.dram_tensor("out", (T, 128, D), F32, kind="ExternalOutput").ap()
    bass_lm_tower(nc, *args, out)
    r = run_bass_kernel_spmd(nc, [arrays], core_ids=[0])
    return r.results[0]["out"]
```
